# Optimizing a Trainium2 kernel written in Bass

```python
import numpy as np
import jax
import jax.numpy as jnp

def _softmax(x, axis=-1):
    return jax.nn.softmax(x, axis=axis)

def _gelu(x):
    return jax.nn.gelu(x, approximate=True)

def _silu(x):
    return jax.nn.silu(x)

def _sigmoid(x):
    return jax.nn.sigmoid(x)

def _layernorm(x, axis=-1, eps=1e-05):
    m = jnp.mean(x, axis=axis, keepdims=True)
    v = jnp.var(x, axis=axis, keepdims=True)
    return (x - m) / jnp.sqrt(v + eps)

def _scatter_add(tgt, idx, src, axis=0):
    return tgt.at[idx].add(src)

def _segment_sum(src, seg, n):
    return jax.ops.segment_sum(src, seg, n)
kernel_name = 'mk_gnn_ffn_d1_gnn_r8_61dbb5'

def setup_inputs(seed: int=0):
    np.random.seed(seed)
    _w = jnp.asarray

    def _rec_inputs():
        import jax
        import jax.numpy as jnp
        _gk = jax.random.key(seed)
        x = -0.0002117 + 1 * jax.random.normal(jax.random.fold_in(_gk, 1), (1250, 512), jnp.float32)
        _s = jax.random.randint(jax.random.fold_in(_gk, 2), (20000,), 0, 1250, jnp.int32)
        _d = jax.random.randint(jax.random.fold_in(_gk, 3), (20000,), 0, 1250, jnp.int32)
        _loop = jnp.arange(1250, dtype=jnp.int32)
        src = jnp.concatenate([_s, _d, _loop])
        dst = jnp.concatenate([_d, _s, _loop])
        _o = jnp.argsort(dst, stable=True)
        src = src[_o]
        dst = dst[_o]
        return (x, src, dst)
    x, src, dst = _rec_inputs()

    def _L0_gnn_setup():
        import jax, jax.numpy as jnp
        import numpy as np
        N = 6250
        E = 200000
        IN_DIM, HID, LAT = (512, 128, 64)
        DEC_DIMS = [128, 256]
        OUT_DIM = 512

        def _glorot(key, shape):
            fan_in, fan_out = (shape[1], shape[0])
            lim = (6.0 / (fan_in + fan_out)) ** 0.5
            return jax.random.uniform(key, shape, jnp.float32, -lim, lim)

        def gcn_conv(x, W, b, src, dst, n):
            h = x @ W.T
            loop = jnp.arange(n, dtype=src.dtype)
            s = jnp.concatenate([src, loop])
            d = jnp.concatenate([dst, loop])
            deg = jnp.zeros((n,), h.dtype).at[d].add(1.0)
            dinv = jnp.where(deg > 0, deg ** (-0.5), 0.0)
            norm = dinv[s] * dinv[d]
            msg = h[s] * norm[:, None]
            out = jax.ops.segment_sum(msg, d, num_segments=n)
            return out + b
        key = jax.random.key(seed)
        ks = jax.random.split(key, 12)
        x = jax.random.normal(ks[0], (N, IN_DIM), jnp.float32)
        edge_index = jax.random.randint(ks[1], (2, E), 0, N, jnp.int64)
        W1 = _glorot(ks[2], (HID, IN_DIM))
        b1 = jnp.zeros((HID,), jnp.float32)
        W2 = _glorot(ks[3], (LAT, HID))
        b2 = jnp.zeros((LAT,), jnp.float32)
        Wd1 = _glorot(ks[4], (DEC_DIMS[0], LAT))
        bd1 = jnp.zeros((DEC_DIMS[0],), jnp.float32)
        Wd2 = _glorot(ks[5], (DEC_DIMS[1], DEC_DIMS[0]))
        bd2 = jnp.zeros((DEC_DIMS[1],), jnp.float32)
        Wd3 = _glorot(ks[6], (OUT_DIM, DEC_DIMS[1]))
        bd3 = jnp.zeros((OUT_DIM,), jnp.float32)
        return dict(x=x, edge_index=edge_index, W1=W1, b1=b1, W2=W2, b2=b2, Wd1=Wd1, bd1=bd1, Wd2=Wd2, bd2=bd2, Wd3=Wd3, bd3=bd3)
    _L0_gnn_all = _L0_gnn_setup()
    _L0_gnn_in = {k: v for k, v in _L0_gnn_all.items() if k in ('W1', 'b1', 'W2', 'b2', 'Wd1', 'bd1', 'Wd2', 'bd2', 'Wd3', 'bd3')}
    del _L0_gnn_all

    def _L0_ffn_setup():
        import jax, jax.numpy as jnp
        import numpy as np
        NUM_EXPERTS = 8
        TOP_K = 2
        key = jax.random.key(seed)
        k0, k1, k2, k3, k4 = jax.random.split(key, 5)
        sl, bs, hs, ffn = (256, 2, 512, 256)
        T = sl * bs
        x = jax.random.normal(k0, (sl, bs, hs), jnp.float32)
        expert_weights = jax.random.uniform(k1, (T, TOP_K), jnp.float32)
        expert_indices = jax.random.randint(k2, (T, TOP_K), 0, NUM_EXPERTS)
        w1 = jax.random.normal(k3, (NUM_EXPERTS, hs, ffn), jnp.float32) * hs ** (-0.5)
        w2 = jax.random.normal(k4, (NUM_EXPERTS, ffn, hs), jnp.float32) * ffn ** (-0.5)
        return dict(x=x, expert_weights=expert_weights, expert_indices=expert_indices, w1=w1, w2=w2)
    _L0_ffn_all = _L0_ffn_setup()
    _L0_ffn_in = {k: v for k, v in _L0_ffn_all.items() if k in ('expert_weights', 'expert_indices', 'w1', 'w2')}
    del _L0_ffn_all
    return {'x': x, 'src': src, 'dst': dst, 'L0_gnn_W1': _L0_gnn_in['W1'], 'L0_gnn_b1': _L0_gnn_in['b1'], 'L0_gnn_W2': _L0_gnn_in['W2'], 'L0_gnn_b2': _L0_gnn_in['b2'], 'L0_gnn_Wd1': _L0_gnn_in['Wd1'], 'L0_gnn_bd1': _L0_gnn_in['bd1'], 'L0_gnn_Wd2': _L0_gnn_in['Wd2'], 'L0_gnn_bd2': _L0_gnn_in['bd2'], 'L0_gnn_Wd3': _L0_gnn_in['Wd3'], 'L0_gnn_bd3': _L0_gnn_in['bd3'], 'L0_ffn_expert_weights': _L0_ffn_in['expert_weights'], 'L0_ffn_expert_indices': _L0_ffn_in['expert_indices'], 'L0_ffn_w1': _L0_ffn_in['w1'], 'L0_ffn_w2': _L0_ffn_in['w2']}

def reference(x, src, dst, L0_gnn_W1, L0_gnn_b1, L0_gnn_W2, L0_gnn_b2, L0_gnn_Wd1, L0_gnn_bd1, L0_gnn_Wd2, L0_gnn_bd2, L0_gnn_Wd3, L0_gnn_bd3, L0_ffn_expert_weights, L0_ffn_expert_indices, L0_ffn_w1, L0_ffn_w2):
    import jax
    import jax.numpy as jnp

    def _L0_gnn_ref(x, edge_index, W1, b1, W2, b2, Wd1, bd1, Wd2, bd2, Wd3, bd3):
        import jax, jax.numpy as jnp
        import numpy as np
        N = 6250
        E = 200000
        IN_DIM, HID, LAT = (512, 128, 64)
        DEC_DIMS = [128, 256]
        OUT_DIM = 512

        def _glorot(key, shape):
            fan_in, fan_out = (shape[1], shape[0])
            lim = (6.0 / (fan_in + fan_out)) ** 0.5
            return jax.random.uniform(key, shape, jnp.float32, -lim, lim)

        def gcn_conv(x, W, b, src, dst, n):
            h = x @ W.T
            loop = jnp.arange(n, dtype=src.dtype)
            s = jnp.concatenate([src, loop])
            d = jnp.concatenate([dst, loop])
            deg = jnp.zeros((n,), h.dtype).at[d].add(1.0)
            dinv = jnp.where(deg > 0, deg ** (-0.5), 0.0)
            norm = dinv[s] * dinv[d]
            msg = h[s] * norm[:, None]
            out = jax.ops.segment_sum(msg, d, num_segments=n)
            return out + b
        src, dst = (edge_index[0], edge_index[1])
        n = x.shape[0]
        h = gcn_conv(x, W1, b1, src, dst, n)
        h = jax.nn.relu(h)
        z = gcn_conv(h, W2, b2, src, dst, n)
        y = jax.nn.relu(z @ Wd1.T + bd1)
        y = jax.nn.relu(y @ Wd2.T + bd2)
        return y @ Wd3.T + bd3

    def _L0_ffn_ref(x, expert_weights, expert_indices, w1, w2):
        import jax, jax.numpy as jnp
        import numpy as np
        NUM_EXPERTS = 8
        TOP_K = 2
        'Dropless MoE: sort assignments by expert, gather tokens, grouped MLP,\n            scatter-combine with top-k router weights (megablocks gather/scatter semantics).'
        in_shape = x.shape
        hs = in_shape[-1]
        x_flat = x.reshape(-1, hs)
        T = x_flat.shape[0]
        flat_ids = expert_indices.reshape(-1)
        order = jnp.argsort(flat_ids)
        bin_ids = flat_ids[order]
        token_ids = order // TOP_K
        xg = x_flat[token_ids]
        y = jnp.zeros_like(xg)
        for e in range(NUM_EXPERTS):
            h = jax.nn.gelu(xg @ w1[e], approximate=False)
            y = jnp.where((bin_ids == e)[:, None], h @ w2[e], y)
        w = expert_weights.reshape(-1)[order][:, None]
        out = jnp.zeros((T, hs), x.dtype).at[token_ids].add(w * y)
        return out.reshape(in_shape)
    edge_index = jnp.stack([src, dst])
    x = x + _L0_gnn_ref(_layernorm(x, axis=-1), edge_index, L0_gnn_W1, L0_gnn_b1, L0_gnn_W2, L0_gnn_b2, L0_gnn_Wd1, L0_gnn_bd1, L0_gnn_Wd2, L0_gnn_bd2, L0_gnn_Wd3, L0_gnn_bd3)
    x = x + _L0_ffn_ref(_layernorm(x, axis=-1)[None], L0_ffn_expert_weights, L0_ffn_expert_indices, L0_ffn_w1, L0_ffn_w2)[0]
    return x

_drawn_inputs = setup_inputs


def setup_inputs(seed=0):
    import zlib

    import numpy as np

    out = dict(_drawn_inputs(seed))
    spreads = {'L0_gnn_b1': (0.0, 0.612),
     'L0_gnn_b2': (0.0, 0.31),
     'L0_gnn_bd1': (0.0, 0.269),
     'L0_gnn_bd2': (0.0, 0.1),
     'L0_gnn_bd3': (0.0, 0.1)}
    factors = {'L0_gnn_W1': 5.068}
    for name, (base, spread) in spreads.items():
        noise = np.random.default_rng([zlib.crc32(name.encode()), seed]).standard_normal(out[name].shape)
        drawn = base * np.exp(spread * noise) if base else spread * noise
        out[name] = jnp.asarray(drawn.astype(out[name].dtype))
    for name, factor in factors.items():
        out[name] = (out[name] * factor).astype(out[name].dtype)
    return out
```

```python
from contextlib import ExitStack

import concourse.bass as bass
from concourse import mybir

ALU = mybir.AluOpType
ACT = mybir.ActivationFunctionType
AX = mybir.AxisListType
F32 = mybir.dt.float32
BF16 = mybir.dt.bfloat16
FP16 = mybir.dt.float16
I32 = mybir.dt.int32

P = 128
EPS = 1e-5


def ceil_div(a, b):
    return -(-a // b)


def gnn_moe(nc, x, src, dst, W1T, b1, W2T, b2, Wd1T, bd1, Wd2T, bd2, Wd3T, bd3, gate_w, gate_i,
            w1, w2, out):
    N, D = x.shape
    E = src.shape[0]
    HID, LAT = W1T.shape[1], W2T.shape[1]
    DEC1, DEC2 = Wd1T.shape[1], Wd2T.shape[1]
    T, TOPK = gate_w.shape
    NE, _, FF = w1.shape
    KD, KF = D // P, FF // P
    CH = ceil_div(N, P)
    TAIL = N - (CH - 1) * P
    NP = CH * P
    TC = T // P
    GROUP = 2
    WINDOW = 12
    COLS = CH * WINDOW
    BATCH = 8
    BG = BATCH // GROUP
    ROWT = 4
    ROWG = ROWT // GROUP
    ROWS = ceil_div(E, ROWT * P)
    TILES = ROWS * ROWT
    GROUPS = TILES // GROUP
    NBATCH = ceil_div(TILES, BATCH)
    RING = 4
    BUILD_BANKS = 4
    NWIN = ceil_div(N, WINDOW)
    FULL = E // (ROWT * P)
    LEFT = E - FULL * ROWT * P
    NO_SOURCE = 8191
    assert BG * COLS <= 512 and T % P == 0 and ROWS <= P and N - 1 + WINDOW <= NP and NWIN * WINDOW <= NP
    assert LEFT > 0 and ROWS == FULL + 1
    HEAD = 12
    assert (NBATCH - 1 - HEAD) % BUILD_BANKS == 0 and HEAD % BUILD_BANKS == 0 and HEAD > CH
    G2_PIECES = [(a, min(a + 512 // LAT, CH)) for a in range(0, CH, 512 // LAT)]
    SPANS = [(a, min(512, NP - a)) for a in range(0, NP, 512)]

    ctx = ExitStack()
    with ctx:
        def sb(name, shape, dt=F32):
            return ctx.enter_context(nc.sbuf_tensor(name, shape, dt))

        def sem(name):
            return ctx.enter_context(nc.semaphore(name))

        bank = [ctx.enter_context(nc.psum_tensor(f"bank{i}", [P, 512], F32)) for i in range(8)]

        x_sb = sb("x_sb", [P, CH, D])
        w1t_sb = sb("w1t_sb", [P, KD, HID])
        w2t_sb = sb("w2t_sb", [HID, LAT])
        wd1t_sb = sb("wd1t_sb", [2 * LAT, DEC1])
        wd2t_sb = sb("wd2t_sb", [DEC1, DEC2])
        wd3t_sb = sb("wd3t_sb", [P, DEC2 // P, D])
        b1_sb = sb("b1_sb", [HID, 1])
        b2_sb = sb("b2_sb", [2 * LAT, 1])
        bd1_sb = sb("bd1_sb", [DEC1, 1])
        bd2_sb = sb("bd2_sb", [P, DEC2 // P])
        bd3_sb = sb("bd3_sb", [P, D])
        gw_sb = sb("gw_sb", [P, TC, TOPK])
        gi_sb = sb("gi_sb", [P, TC, TOPK], I32)
        ew1 = sb("ew1", [P, NE, KD, FF])
        ew2 = sb("ew2", [P, NE, KF, D])

        at = sb("at", [P, CH, NP], BF16)
        at2 = sb("at2", [P, CH, NP], BF16)
        at_flat = at[:, :, :].rearrange("p c n -> p (c n)").bitcast(F32)
        at2_flat = at2[:, :, :].rearrange("p c n -> p (c n)").bitcast(F32)
        rowlen = ROWT * P
        edges = at2_flat[0:ROWS, 0:2 * rowlen].rearrange("p (k e) -> p k e", k=2).bitcast(I32)
        frow = at2_flat[0:ROWS, 2 * rowlen:4 * rowlen].rearrange("p (k e) -> p k e", k=2)
        y1t = at2_flat[:, 0:NP]
        y2t = at2_flat[:, NP:3 * NP].rearrange("p (k n) -> p k n", k=2)
        hidden = at_flat[:, 0:2 * KF * T].rearrange("p (b k t) -> p b k t", b=2, k=KF)

        ring = sb("ring", [P, RING * BATCH * (P + COLS)], BF16)
        n_src = RING * BATCH * P
        hot_src = ring[:, 0:n_src].rearrange("p (r t n) -> p r t n", r=RING, t=BATCH)
        hot_dst = ring[:, n_src:].rearrange("p (r t n) -> p r t n", r=RING, t=BATCH)
        part = ring[:, 0:3 * NP].rearrange("p (k c n) -> p k c n", k=3, c=CH)
        rest = ring[:, 3 * NP:5 * NP].bitcast(F32).rearrange("p (c n) -> p c n", c=CH)
        part2 = ring[:, 0:NP].rearrange("p (c n) -> p c n", c=CH)
        part3 = ring[:, NP:2 * NP].rearrange("p (c n) -> p c n", c=CH)
        rest2 = rest[:, :, 0:LAT]

        TP = NBATCH * BATCH
        src_lo = sb("src_lo", [P, TP])
        key = sb("key", [P, TP])
        hi_win = sb("hi_win", [P, TP])
        rel = sb("rel", [P, TP])
        isrc = at2_flat[:, 4 * rowlen:4 * rowlen + 3 * TILES].rearrange("p (k t) -> p k t", k=3).bitcast(I32)
        carry_key = sb("carry_key", [P, GROUPS])
        hot_carry = sb("hot_carry", [P, GROUPS, CH], BF16)
        gstat = sb("gstat", [P, 4, ROWG])
        gall = sb("gall", [P, 4, GROUPS])
        first_i = sb("first_i", [1, GROUPS], I32)
        viol = sb("viol", [P, 4, GROUPS])
        n_viol = sb("n_viol", [P, 8])
        slow_i = sb("slow_i", [1, 1], I32)
        base_t = sb("base_t", [P, 1])

        xnt = sb("xnt", [P, KD, NP])
        xnt_flat = xnt[:, :, :].rearrange("p k n -> p (k n)")
        h1t = xnt_flat[:, 0:NP]
        zt = xnt_flat[:, NP:2 * NP]
        xn2t = xnt_flat[:, 2 * NP:2 * NP + KD * T].rearrange("p (k t) -> p k t", k=KD)
        dinv_row = xnt_flat[:, 2 * NP:3 * NP]
        std_row = xnt_flat[:, 3 * NP:4 * NP]
        xn = sb("xn", [P, 2, D])
        skey = xn[:, :, :].rearrange("p a n -> p (a n)")[:, 0:3 * TP].rearrange("p (k t) -> p k t", k=3)

        iota_lanes = sb("iota_lanes", [P, P], FP16)
        ident = sb("ident", [P, P])
        ident_bf = sb("ident_bf", [P, P], BF16)
        ones_bf = sb("ones_bf", [P, P], BF16)
        zeros_bf = sb("zeros_bf", [P, COLS], BF16)
        one = sb("one", [P, 1])
        eps = sb("eps", [P, 1])

        stats = sb("stats", [P, CH, 6])
        mv = sb("mv", [P, CH, 2])
        rstd = sb("rstd", [P, 2, CH])
        h_sb = sb("h_sb", [P, CH, HID])
        dinv_col = sb("dinv_col", [P, CH])
        gate = sb("gate", [P, TC, NE])
        gate_part = sb("gate_part", [P, 2, TC, NE])
        gif = sb("gif", [P, TC, TOPK])
        expert_no = sb("expert_no", [P, NE])

        s_edges = sem("s_edges")
        s_edge_pad = sem("s_edge_pad")
        s_x = [sem(f"s_x_chunk{c}") for c in range(CH)]
        s_xpad = sem("s_xpad")
        s_at_zero = sem("s_at_zero")
        s_wg = sem("s_wg")
        s_gates = sem("s_gates")
        s_ew = sem("s_ew")
        s_const = sem("s_const")
        s_dve = sem("s_dve")
        s_rows = sem("s_rows")
        s_rowT = sem("s_rowT")
        s_ready = sem("s_ready")
        s_carry = sem("s_carry")
        s_summed = sem("s_summed")
        s_placed = sem("s_placed")
        s_first = sem("s_first")
        s_slow = sem("s_slow")
        s_mv = sem("s_mv")
        s_std = sem("s_std")
        s_rstd = sem("s_rstd")
        s_xn = sem("s_xn")
        s_xnT = sem("s_xnT")
        s_xnt = sem("s_xnt")
        s_h = sem("s_h")
        s_hsb = sem("s_hsb")
        s_gen_begin = sem("s_gen_begin")
        s_gen_dve = sem("s_gen_dve")
        s_gen_free = sem("s_gen_free")
        s_gen_ready = sem("s_gen_ready")
        s_gen_used = sem("s_gen_used")
        s_gen_sum = sem("s_gen_sum")
        s_gen_at = sem("s_gen_at")
        s_gen_at2 = sem("s_gen_at2")
        s_deg = sem("s_deg")
        s_deg_std = sem("s_deg_std")
        s_dinv_row = sem("s_dinv_row")
        s_dinvT = sem("s_dinvT")
        s_dinv = sem("s_dinv")
        s_p0 = sem("s_p0")
        s_r0 = sem("s_r0")
        s_p1 = sem("s_p1")
        s_p2 = sem("s_p2")
        s_agg1 = sem("s_agg1")
        s_agg1s = sem("s_agg1s")
        s_h1t = sem("s_h1t")
        s_h2 = sem("s_h2")
        s_g2 = sem("s_g2")
        s_q0 = sem("s_q0")
        s_q0r = sem("s_q0r")
        s_q1 = sem("s_q1")
        s_q2 = sem("s_q2")
        s_q2_pad = sem("s_q2_pad")
        s_agg2 = sem("s_agg2")
        s_agg2s = sem("s_agg2s")
        s_zt = sem("s_zt")
        s_d1 = sem("s_d1")
        s_y1 = sem("s_y1")
        s_d2 = sem("s_d2")
        s_y2 = sem("s_y2")
        s_d3 = sem("s_d3")
        s_x2 = sem("s_x2")
        s_mv2 = sem("s_mv2")
        s_std2 = sem("s_std2")
        s_rstd2 = sem("s_rstd2")
        s_xn2 = sem("s_xn2")
        s_xn2T = sem("s_xn2T")
        s_xn2t = sem("s_xn2t")
        s_up = sem("s_up")
        s_gelu = sem("s_gelu")
        s_down = sem("s_down")
        s_acc = sem("s_acc")
        s_out = sem("s_out")
        s_out_rest = sem("s_out_rest")

        block = ctx.enter_context(nc.Block())
        NCONST = 11
        NWG = 11
        HALF = ceil_div(CH, 2)
        HALVES = [(0, HALF), (HALF, CH)]

        def is_slow(eng):
            eng.wait_ge(s_slow, 1)
            _, (v,) = nc.values_load_multi_w_load_instructions(
                slow_i[0:1, 0:1], engines=[eng.engine], min_val=0, max_val=1,
                skip_runtime_bounds_check_because="the flag is clamped to 0 and 1 when it is made")
            return v

        @block.sync
        def _(sp):
            sp.wait_ge(s_edge_pad, 2)
            for k, a in enumerate((src, dst)):
                sp.dma_start(edges[0:FULL, k, :],
                             a[0:FULL * rowlen].rearrange("(r e) -> r e", e=rowlen)).then_inc(s_edges, 16)
                sp.dma_start(edges[FULL:ROWS, k, 0:LEFT],
                             a[FULL * rowlen:E].rearrange("(a e) -> a e", a=1)).then_inc(s_edges, 16)
            for c in range(CH):
                n = P if c < CH - 1 else TAIL
                if n < P:
                    sp.wait_ge(s_xpad, 1)
                sp.dma_start(x_sb[0:n, c, :], x[c * P:c * P + n, :]).then_inc(s_x[c], 16)
            for e in range(NE):
                sp.dma_start(ew1[:, e], w1[e].rearrange("(k p) n -> p k n", p=P)).then_inc(s_ew, 16)
                sp.dma_start(ew2[:, e], w2[e].rearrange("(k p) n -> p k n", p=P)).then_inc(s_ew, 16)
            for c in range(TC, CH):
                n = P if c < CH - 1 else TAIL
                sp.wait_ge(s_x2, c + 1)
                sp.dma_start(out[c * P:c * P + n, :], x_sb[0:n, c, :]).then_inc(s_out_rest, 16)
            for c in range(TC):
                sp.wait_ge(s_acc, TC * (NE - 1) + c + 1)
                sp.dma_start(out[c * P:(c + 1) * P, :], x_sb[:, c, :]).then_inc(s_out, 16)
            sp.wait_ge(s_out_rest, 16 * (CH - TC))
            sp.wait_ge(s_out, 16 * TC)

        @block.gpsimd
        def _(pool):
            nc.gpsimd.memset(edges[:, 0, :], NO_SOURCE).then_inc(s_edge_pad, 1)
            nc.gpsimd.memset(edges[:, 1, :], N).then_inc(s_edge_pad, 1)
            nc.gpsimd.memset(ident[:, :], 0.0).then_inc(s_const, 1)
            nc.gpsimd.memset(ident_bf[:, :], 0.0).then_inc(s_const, 1)
            pool.wait_ge(s_const, 2)
            for m in (ident, ident_bf):
                nc.gpsimd.affine_select(out=m[:, :], in_=m[:, :], compare_op=ALU.not_equal, fill=1.0, base=0,
                                        pattern=[[-1, P]], channel_multiplier=1).then_inc(s_const, 1)
            nc.gpsimd.iota(iota_lanes[:, :], pattern=[[1, P]], base=0, channel_multiplier=0,
                           allow_small_or_imprecise_dtypes=True).then_inc(s_const, 1)
            nc.gpsimd.iota(expert_no[:, :], pattern=[[1, NE]], base=0, channel_multiplier=0,
                           allow_small_or_imprecise_dtypes=True).then_inc(s_const, 1)
            nc.gpsimd.memset(eps[:, :], EPS).then_inc(s_const, 1)
            nc.gpsimd.memset(one[:, :], 1.0).then_inc(s_const, 1)
            nc.gpsimd.memset(ones_bf[:, :], 1.0).then_inc(s_const, 1)
            nc.gpsimd.memset(b2_sb[:, :], 0.0).then_inc(s_const, 1)
            nc.gpsimd.memset(zeros_bf[:, :], 0.0).then_inc(s_const, 1)
            nc.gpsimd.memset(x_sb[:, CH - 1, :], 0.0).then_inc(s_xpad, 1)
            nc.gpsimd.memset(at_flat, 0.0).then_inc(s_at_zero, 1)
            pool.wait_ge(s_agg1, len(SPANS))
            nc.gpsimd.memset(part3[:, :, LAT:], 0.0).then_inc(s_q2_pad, 1)

        @block.vector
        def _(dve):
            chain = [0]

            def link(ins):
                chain[0] += 1
                ins.then_inc(s_dve, 1)
                dve.wait_ge(s_dve, chain[0])

            v = nc.vector
            dve.wait_ge(s_edges, 64)
            glen = GROUP * P
            i_dst = edges[:, 1, :].rearrange("p (h e) -> p h e", h=ROWG)
            v.tensor_copy(frow[:, 0, :], edges[:, 0, :])
            link(v.tensor_reduce(gstat[0:ROWS, 0], i_dst, AX.X, ALU.min))
            for h in range(ROWG):
                last = v.tensor_scalar(frow[:, 1, h * glen:(h + 1) * glen], edges[:, 1, h * glen:(h + 1) * glen],
                                       gstat[0:ROWS, 0, h:h + 1], None, ALU.subtract)
            v.tensor_reduce(gstat[0:ROWS, 1], i_dst, AX.X, ALU.max)
            v.tensor_reduce(gstat[0:ROWS, 2], i_dst[:, :, 0:glen - P], AX.X, ALU.max)
            v.tensor_reduce(gstat[0:ROWS, 3], i_dst[:, :, glen - P:glen], AX.X, ALU.min).then_inc(s_rows, 1)
            v.memset(key[:, TILES:TP], -1.0)
            v.memset(src_lo[:, TILES:TP], 0.0)
            link(v.memset(hi_win[:, TILES:TP], 0.0))

            for c in range(CH):
                dve.wait_ge(s_x[c], 16)
                link(v.bn_stats(stats[:, c], x_sb[:, c]))
                last = v.bn_aggr(mv[:, c], stats[:, c])
            last.then_inc(s_mv, 1)

            dve.wait_ge(s_rowT, 1)

            def by_tile(bank_, width=TILES):
                return bank_[:, 0:width].rearrange("p (t r) -> p r t", t=ROWT)

            v.tensor_copy(gall[:, 0:3], bank[2][:, 0:3 * GROUPS].rearrange("p (k g) -> p k g", k=3))
            v.tensor_copy(rel[:, 0:TILES].rearrange("p (r t) -> p r t", t=ROWT), by_tile(bank[1]))
            link(v.tensor_copy(isrc[:, 0, :].rearrange("p (r t) -> p r t", t=ROWT), by_tile(bank[0])))
            v.tensor_scalar(isrc[:, 1], isrc[:, 0], P - 1, None, ALU.bitwise_and)
            link(v.tensor_scalar(isrc[:, 2], isrc[:, 0], 7, None, ALU.arith_shift_right))
            v.tensor_copy(src_lo[:, 0:TILES], isrc[:, 1])
            link(v.tensor_scalar(hi_win[:, 0:TILES], isrc[:, 2], float(WINDOW), None, ALU.mult))
            v.tensor_copy(first_i[:, :], gall[0:1, 0]).then_inc(s_first, 1)
            v.tensor_tensor(viol[:, 0, 0:GROUPS - 1], gall[:, 0, 1:GROUPS], gall[:, 0, 0:GROUPS - 1], ALU.subtract)
            link(v.tensor_tensor(key[:, 0:TILES], hi_win[:, 0:TILES], rel[:, 0:TILES], ALU.add))

            def one_hots(slot, lo, hi, lanes):
                n = BATCH
                v.tensor_tensor(hot_src[:, slot], iota_lanes[:, :].unsqueeze(1).to_broadcast([P, n, P]),
                                lo.unsqueeze(2).to_broadcast([P, n, P]), ALU.is_equal)
                return v.tensor_tensor(hot_dst[:, slot], lanes.unsqueeze(1).to_broadcast([P, n, COLS]),
                                       hi.unsqueeze(2).to_broadcast([P, n, COLS]), ALU.is_equal)

            dve.wait_ge(s_const, NCONST)
            for b in range(NBATCH):
                if b >= RING - 1:
                    dve.wait_ge(s_summed, b - RING + 2)
                t0 = b * BATCH
                one_hots(b % RING, src_lo[:, t0:t0 + BATCH], key[:, t0:t0 + BATCH],
                         iota_lanes[:, 0:COLS]).then_inc(s_ready, 1)
                if b == 0:
                    link(v.tensor_tensor(viol[:, 1, 0:GROUPS - 1],
                                         rel[:, 0:TILES].rearrange("p (g t) -> p g t", t=GROUP)[:, 0:GROUPS - 1, GROUP - 1],
                                         viol[:, 0, 0:GROUPS - 1], ALU.is_equal))
                    link(v.scalar_tensor_tensor(carry_key[:, 0:GROUPS - 1],
                                                hi_win[:, 0:TILES].rearrange("p (g t) -> p g t", t=GROUP)[:, 0:GROUPS - 1, GROUP - 1],
                                                1.0, viol[:, 1, 0:GROUPS - 1], ALU.add, ALU.mult))
                    v.tensor_tensor(hot_carry[:, 0:GROUPS - 1],
                                    iota_lanes[:, 1:COLS + 1:WINDOW].unsqueeze(1).to_broadcast([P, GROUPS - 1, CH]),
                                    carry_key[:, 0:GROUPS - 1].unsqueeze(2).to_broadcast([P, GROUPS - 1, CH]),
                                    ALU.is_equal).then_inc(s_carry, 1)
                if b == 1:
                    dve.wait_ge(s_std, 1)
                    dve.wait_ge(s_mv, 1)
                    link(v.reciprocal(rstd[:, 0], rstd[:, 1]))
                    v.scalar_tensor_tensor(rstd[:, 1], mv[:, :, 0], -1.0, rstd[:, 0], ALU.mult, ALU.mult).then_inc(s_rstd, 1)
                if b == 2:
                    dve.wait_ge(s_carry, 1)
                    v.tensor_copy(gall[:, 3], bank[3][:, 0:GROUPS])
                    link(v.memset(viol[:, 1:4, GROUPS - 1:GROUPS], 0.0))
                    link(v.tensor_tensor(viol[:, 0], gall[:, 1], gall[:, 0], ALU.subtract))
                    link(v.tensor_scalar(viol[:, 0], viol[:, 0], float(WINDOW) - 0.5, None, ALU.is_gt))
                    v.tensor_tensor(viol[:, 1, 0:GROUPS - 1], gall[:, 1, 0:GROUPS - 1], gall[:, 0, 1:GROUPS], ALU.is_gt)
                    v.tensor_tensor(viol[:, 2, 0:GROUPS - 1], gall[:, 2, 0:GROUPS - 1], gall[:, 0, 1:GROUPS], ALU.is_ge)
                    link(v.tensor_tensor(viol[:, 3], gall[:, 3], gall[:, 0], ALU.is_le))
                    link(v.tensor_reduce(n_viol[:, 0:1], viol[:, :, :].rearrange("p a b -> p (a b)"), AX.X, ALU.max))
                    v.tensor_copy(slow_i[:, :], n_viol[0:1, 0:1]).then_inc(s_slow, 1)

            slow = is_slow(dve)
            with dve.If(slow != 0):
                dve.wait_ge(s_summed, NBATCH)
                dve.wait_ge(s_placed, GROUPS)
                v.memset(base_t[:, :], 0.0)
                v.memset(skey[:, 0, TILES:TP], -float(2 * NP))
                v.tensor_tensor(skey[:, 0, 0:TILES].rearrange("p (g t) -> p g t", t=GROUP),
                                rel[:, 0:TILES].rearrange("p (g t) -> p g t", t=GROUP),
                                gall[:, 0].unsqueeze(2).to_broadcast([P, GROUPS, GROUP]), ALU.add).then_inc(s_gen_begin, 1)
                dve.wait_ge(s_gen_begin, 1)
                steps = 6
                with dve.Fori(0, NWIN) as w:
                    turn = [0]

                    def again(ins):
                        turn[0] += 1
                        ins.then_inc(s_gen_dve, 1)
                        dve.wait_ge(s_gen_dve, w * steps + turn[0])

                    again(v.tensor_scalar(skey[:, 1], skey[:, 0], base_t[:, :], None, ALU.subtract))
                    again(v.tensor_scalar(skey[:, 2], skey[:, 1], float(WINDOW), None, ALU.is_lt))
                    again(v.scalar_tensor_tensor(skey[:, 2], skey[:, 1], 0.0, skey[:, 2], ALU.is_ge, ALU.mult))
                    again(v.scalar_tensor_tensor(skey[:, 1], skey[:, 1], 1.0, hi_win[:, :], ALU.add, ALU.add))
                    again(v.tensor_tensor(skey[:, 1], skey[:, 1], skey[:, 2], ALU.mult))
                    v.tensor_scalar(base_t[:, :], base_t[:, :], float(WINDOW), None, ALU.add).then_inc(s_gen_dve, 1)
                    with dve.Fori(0, NBATCH) as b:
                        dve.wait_ge(s_gen_dve, w * steps + steps)
                        dve.wait_ge(s_gen_used, w * NBATCH + b + 1)
                        one_hots(0, src_lo[:, bass.ds(b * BATCH, BATCH)], skey[:, 1, bass.ds(b * BATCH, BATCH)],
                                 iota_lanes[:, 1:COLS + 1]).then_inc(s_gen_ready, 1)
                    dve.wait_ge(s_gen_at, w + 1)
                    v.tensor_tensor(at2[:, :, bass.ds(w * WINDOW, WINDOW)], bank[0][:, 0:COLS].rearrange("p (c n) -> p c n", c=CH),
                                    at[:, :, bass.ds(w * WINDOW, WINDOW)], ALU.subtract).then_inc(s_gen_at2, 1)
                dve.wait_ge(s_gen_at2, NWIN)

            for i, (a, n) in enumerate(SPANS):
                dve.wait_ge(s_deg_std, i + 1)
                v.reciprocal(dinv_row[:, a:a + n], std_row[:, a:a + n]).then_inc(s_dinv_row, 1)
            dve.wait_ge(s_dinvT, 1)
            v.tensor_copy(dinv_col[:, :], bank[3][:, 0:CH]).then_inc(s_dinv, 1)
            dve.wait_ge(s_dinv, 1)
            for i, (a, b) in enumerate(HALVES):
                for c in range(a, b):
                    dve.wait_ge(s_p0, c + 1)
                    last = v.scalar_tensor_tensor(rest[:, c], h_sb[:, c], dinv_col[:, c:c + 1], part[:, 0, c],
                                                  ALU.mult, ALU.subtract)
                last.then_inc(s_r0, 1)
            for i, (a, b) in enumerate(HALVES):
                dve.wait_ge(s_p1, i + 1)
                v.tensor_tensor(part[:, 2, a:b], rest[:, a:b], part[:, 1, a:b], ALU.subtract).then_inc(s_p2, 1)
            for i, (a, n) in enumerate(SPANS):
                dve.wait_ge(s_agg1, i + 1)
                v.tensor_tensor(h1t[:, a:a + n], bank[4 + i][:, 0:n], dinv_row[:, a:a + n], ALU.mult).then_inc(s_agg1s, 1)
            g2 = h_sb[:, :, 0:LAT]
            for i, (a, b) in enumerate(G2_PIECES):
                dve.wait_ge(s_h2, i + 1)
                v.tensor_tensor(g2[:, a:b], bank[i][:, 0:(b - a) * LAT].rearrange("p (c n) -> p c n", n=LAT),
                                dinv_col[:, a:b].unsqueeze(2).to_broadcast([P, b - a, LAT]), ALU.mult).then_inc(s_g2, 1)
            dve.wait_ge(s_g2, len(G2_PIECES))
            dve.wait_ge(s_q0, 1)
            v.tensor_tensor(rest2, g2, part2[:, :, 0:LAT], ALU.subtract).then_inc(s_q0r, 1)
            dve.wait_ge(s_q0r, 1)
            dve.wait_ge(s_q1, 1)
            v.tensor_tensor(part3[:, :, 0:LAT], rest2, part2[:, :, LAT:2 * LAT], ALU.subtract).then_inc(s_q2, 1)
            for i, (a, n) in enumerate(SPANS):
                dve.wait_ge(s_agg2, i + 1)
                v.tensor_tensor(zt[:, a:a + n], bank[4 + i][:, 0:n], dinv_row[:, a:a + n], ALU.mult).then_inc(s_agg2s, 1)

            dve.wait_ge(s_gates, 32)
            dve.wait_ge(s_wg, 16 * NWG)
            v.tensor_copy(gif[:, :, :], gi_sb[:, :, :])
            for c in range(CH):
                last = v.tensor_tensor(x_sb[:, c], x_sb[:, c], bd3_sb[:, :], ALU.add)
            link(last)
            for c in range(TC):
                for k in range(TOPK):
                    last = v.tensor_scalar(gate_part[:, k, c], expert_no[:, :], gif[:, c, k:k + 1], gw_sb[:, c, k:k + 1],
                                           ALU.is_equal, ALU.mult)
            link(last)
            link(v.tensor_tensor(gate[:, :, :], gate_part[:, 0], gate_part[:, 1], ALU.add))
            for c in range(CH):
                dve.wait_ge(s_d3, c + 1)
                v.tensor_tensor(x_sb[:, c], x_sb[:, c], bank[4 + c % 4][:, 0:D], ALU.add).then_inc(s_x2, 1)
                if c < TC:
                    dve.wait_ge(s_x2, c + 1)
                    link(v.bn_stats(stats[:, c], x_sb[:, c]))
                    ins = v.bn_aggr(mv[:, c], stats[:, c])
                    if c == TC - 1:
                        ins.then_inc(s_mv2, 1)
                        dve.wait_ge(s_mv2, 1)
                        dve.wait_ge(s_std2, 1)
                        link(v.reciprocal(rstd[:, 0, 0:TC], rstd[:, 1, 0:TC]))
                        v.scalar_tensor_tensor(rstd[:, 1, 0:TC], mv[:, 0:TC, 0], -1.0, rstd[:, 0, 0:TC],
                                               ALU.mult, ALU.mult).then_inc(s_rstd2, 1)
            for e in range(NE):
                for c in range(TC):
                    i = e * TC + c
                    dve.wait_ge(s_down, i + 1)
                    if e:
                        dve.wait_ge(s_acc, i - TC + 1)
                    v.scalar_tensor_tensor(x_sb[:, c], bank[4 + i % 4][:, 0:D], gate[:, c, e:e + 1], x_sb[:, c],
                                           ALU.mult, ALU.add).then_inc(s_acc, 1)

        @block.scalar
        def _(act):
            act.dma_start(w1t_sb[:, :, :], W1T.rearrange("(k p) n -> p k n", p=P)).then_inc(s_wg, 16)
            act.dma_start(w2t_sb[:, :], W2T).then_inc(s_wg, 16)
            for k in range(2):
                act.dma_start(wd1t_sb[k * LAT:(k + 1) * LAT, :], Wd1T).then_inc(s_wg, 16)
            act.dma_start(wd2t_sb[:, :], Wd2T).then_inc(s_wg, 16)
            act.dma_start(wd3t_sb[:, :, :], Wd3T.rearrange("(k p) n -> p k n", p=P)).then_inc(s_wg, 16)
            act.dma_start(b1_sb[:, :], b1.rearrange("(p a) -> p a", a=1)).then_inc(s_wg, 16)
            act.dma_start(bd1_sb[:, :], bd1.rearrange("(p a) -> p a", a=1)).then_inc(s_wg, 16)
            act.dma_start(bd2_sb[:, :], bd2).then_inc(s_wg, 16)
            act.dma_start(bd3_sb[:, :], bd3.rearrange("(a n) -> a n", a=1).to_broadcast([P, D])).then_inc(s_wg, 16)
            act.wait_ge(s_const, NCONST)
            act.dma_start(b2_sb[0:LAT, :], b2.rearrange("(p a) -> p a", a=1)).then_inc(s_wg, 16)
            act.dma_start(gw_sb[:, :, :], gate_w.rearrange("(c p) k -> p c k", p=P)).then_inc(s_gates, 16)
            act.dma_start(gi_sb[:, :, :], gate_i.rearrange("(c p) k -> p c k", p=P)).then_inc(s_gates, 16)

            def normalise(c):
                if c >= 2:
                    act.wait_ge(s_xnT, c - 1)
                nc.scalar.activation(xn[:, c % 2], x_sb[:, c], ACT.Identity, scale=rstd[:, 0, c:c + 1],
                                     bias=rstd[:, 1, c:c + 1]).then_inc(s_xn, 1)

            def keep_transposed(c):
                act.wait_ge(s_xnT, c + 1)
                nc.scalar.copy(xnt[:, :, c * P:(c + 1) * P],
                               bank[4 + c % 2][:, :].rearrange("p (k n) -> p k n", k=KD)).then_inc(s_xnt, 1)

            def keep_h(c):
                act.wait_ge(s_h, c + 1)
                nc.scalar.copy(h_sb[:, c], bank[6 + c % 2][:, 0:HID]).then_inc(s_hsb, 1)

            def place(b, j, groups=BG):
                act.wait_ge(s_summed, b + 1)
                _, at_col = nc.values_load_multi_w_load_instructions(
                    first_i[0:1, bass.ds(b * BG, groups)], engines=[act.engine], min_val=0, max_val=N - 1,
                    skip_runtime_bounds_check_because="targets are node numbers")
                for g in range(groups):
                    if not (isinstance(b, int) and b + g == 0):
                        act.wait_ge(s_placed, b * BG + g)
                    nc.scalar.copy(at[:, :, bass.ds(at_col[g], WINDOW)],
                                   bank[j][:, g * COLS:(g + 1) * COLS].rearrange("p (c n) -> p c n", c=CH)).then_inc(s_placed, 1)

            act.wait_ge(s_mv, 1)
            nc.scalar.activation(rstd[:, 1], mv[:, :, 1], ACT.Sqrt, bias=eps[:, :]).then_inc(s_std, 1)
            act.wait_ge(s_rstd, 1)
            normalise(0)
            act.wait_ge(s_first, 1)
            act.wait_ge(s_at_zero, 1)
            for b in range(HEAD):
                if b + 1 < CH:
                    normalise(b + 1)
                if b < CH:
                    keep_transposed(b)
                if 1 <= b <= CH:
                    keep_h(b - 1)
                place(b, b % BUILD_BANKS)
            with act.Fori(0, (NBATCH - 1 - HEAD) // BUILD_BANKS) as it:
                for j in range(BUILD_BANKS):
                    place(it * BUILD_BANKS + (HEAD + j), j)
            place(NBATCH - 1, (NBATCH - 1) % BUILD_BANKS, GROUPS - (NBATCH - 1) * BG)

            slow = is_slow(act)
            with act.If(slow != 0):
                with act.Fori(0, NWIN) as w:
                    act.wait_ge(s_gen_sum, w + 1)
                    nc.scalar.copy(at[:, :, bass.ds(w * WINDOW, WINDOW)],
                                   bank[0][:, 0:COLS].rearrange("p (c n) -> p c n", c=CH)).then_inc(s_gen_at, 1)

            for i, (a, n) in enumerate(SPANS):
                act.wait_ge(s_deg, i + 1)
                nc.scalar.activation(std_row[:, a:a + n], bank[i][:, 0:n], ACT.Sqrt, bias=one[:, :]).then_inc(s_deg_std, 1)
            act.wait_ge(s_dinv, 1)
            act.wait_ge(s_hsb, CH)
            for c in range(CH):
                nc.scalar.activation(part[:, 0, c], h_sb[:, c], ACT.Copy, scale=dinv_col[:, c:c + 1]).then_inc(s_p0, 1)
            for i, (a, b) in enumerate(HALVES):
                act.wait_ge(s_r0, i + 1)
                nc.scalar.copy(part[:, 1, a:b], rest[:, a:b]).then_inc(s_p1, 1)
            for i, (a, n) in enumerate(SPANS):
                act.wait_ge(s_agg1s, i + 1)
                nc.scalar.activation(h1t[:, a:a + n], h1t[:, a:a + n], ACT.Relu, bias=b1_sb[:, :]).then_inc(s_h1t, 1)
            act.wait_ge(s_g2, len(G2_PIECES))
            nc.scalar.copy(part2[:, :, 0:LAT], h_sb[:, :, 0:LAT]).then_inc(s_q0, 1)
            act.wait_ge(s_q0r, 1)
            nc.scalar.copy(part2[:, :, LAT:2 * LAT], rest2).then_inc(s_q1, 1)
            for i, (a, n) in enumerate(SPANS):
                act.wait_ge(s_agg2s, i + 1)
                nc.scalar.activation(zt[:, a:a + n], zt[:, a:a + n], ACT.Identity, bias=b2_sb[:, :]).then_inc(s_zt, 1)
            for i, (a, n) in enumerate(SPANS):
                act.wait_ge(s_d1, i + 1)
                nc.scalar.activation(y1t[:, a:a + n], bank[3][:, 0:n], ACT.Relu, bias=bd1_sb[:, :]).then_inc(s_y1, 1)
                for k in range(2):
                    act.wait_ge(s_d2, 2 * i + k + 1)
                    nc.scalar.activation(y2t[:, k, a:a + n], bank[k][:, 0:n], ACT.Relu, bias=bd2_sb[:, k:k + 1]).then_inc(s_y2, 1)
            act.wait_ge(s_mv2, 1)
            nc.scalar.activation(rstd[:, 1, 0:TC], mv[:, 0:TC, 1], ACT.Sqrt, bias=eps[:, :]).then_inc(s_std2, 1)
            act.wait_ge(s_rstd2, 1)
            for c in range(TC):
                if c >= 2:
                    act.wait_ge(s_xn2T, c - 1)
                nc.scalar.activation(xn[:, c % 2], x_sb[:, c], ACT.Identity, scale=rstd[:, 0, c:c + 1],
                                     bias=rstd[:, 1, c:c + 1]).then_inc(s_xn2, 1)
            for c in range(TC):
                act.wait_ge(s_xn2T, c + 1)
                nc.scalar.copy(xn2t[:, :, c * P:(c + 1) * P],
                               bank[c][:, :].rearrange("p (k n) -> p k n", k=KD)).then_inc(s_xn2t, 1)
            for e in range(NE):
                for k in range(KF):
                    act.wait_ge(s_up, KF * e + k + 1)
                    if e >= 2:
                        act.wait_ge(s_down, TC * (e - 1))
                    nc.scalar.activation(hidden[:, e % 2, k], bank[(KF * e + k) % 4][:, 0:T], ACT.Gelu).then_inc(s_gelu, 1)

        @block.tensor
        def _(pe):
            mm = nc.tensor.matmul
            pe.wait_ge(s_const, NCONST)
            pe.wait_ge(s_rows, 1)
            for k in range(2):
                for t in range(ROWT):
                    nc.tensor.transpose(bank[k][:, t * ROWS:(t + 1) * ROWS], frow[:, k, t * P:(t + 1) * P], ident[0:ROWS, 0:ROWS])
            for k in range(4):
                o = bank[2 + k // 3][:, (k % 3) * GROUPS:(k % 3 + 1) * GROUPS].rearrange("p (r h) -> p h r", h=ROWG)
                for h in range(ROWG):
                    last = mm(o[:, h], gstat[0:ROWS, k, h:h + 1].to_broadcast([ROWS, P]), ident[0:ROWS, 0:ROWS],
                              start=True, stop=True)
            last.then_inc(s_rowT, 1)
            pe.wait_ge(s_wg, 16 * NWG)

            def transpose_features(c):
                pe.wait_ge(s_xn, c + 1)
                if c >= 2:
                    pe.wait_ge(s_xnt, c - 1)
                for k in range(KD):
                    last = nc.tensor.transpose(bank[4 + c % 2][:, k * P:(k + 1) * P], xn[:, c % 2, k * P:(k + 1) * P], ident[:, :])
                last.then_inc(s_xnT, 1)

            def project(c):
                pe.wait_ge(s_xnt, c + 1)
                if c >= 2:
                    pe.wait_ge(s_hsb, c - 1)
                for k in range(KD):
                    last = mm(bank[6 + c % 2][:, 0:HID], xnt[:, k, c * P:(c + 1) * P], w1t_sb[:, k],
                              start=(k == 0), stop=(k == KD - 1))
                last.then_inc(s_h, 1)

            for b in range(NBATCH):
                if b < CH:
                    transpose_features(b)
                if 1 <= b <= CH:
                    project(b - 1)
                pe.wait_ge(s_ready, b + 1)
                if b >= BUILD_BANKS:
                    pe.wait_ge(s_placed, BG * (b - BUILD_BANKS + 1))
                if b == 3:
                    pe.wait_ge(s_slow, 1)
                for j in range(min(BG, GROUPS - b * BG)):
                    g = b * BG + j
                    acc = bank[b % BUILD_BANKS][:, j * COLS:(j + 1) * COLS]
                    for t in range(GROUP):
                        last = mm(acc, hot_src[:, b % RING, j * GROUP + t], hot_dst[:, b % RING, j * GROUP + t],
                                  start=(t == 0), stop=(g == 0 and t == GROUP - 1))
                    if g == 1:
                        pe.wait_ge(s_carry, 1)
                    if g >= 1:
                        p = g * GROUP - 1
                        last = mm(acc.rearrange("p (c n) -> p c n", n=WINDOW)[:, :, 0], hot_src[:, p // BATCH % RING, p % BATCH],
                                  hot_carry[:, g - 1], start=False, stop=True)
                last.then_inc(s_summed, 1)

            slow = is_slow(pe)
            pe.wait_ge(s_placed, GROUPS)
            with pe.If(slow != 0):
                pe.wait_ge(s_gen_begin, 1)
                pe.sem_inc(s_gen_used, 1)
                pe.sem_inc(s_gen_free, 1)
                with pe.Fori(0, NWIN) as w:
                    pe.wait_ge(s_gen_free, w + 1)
                    mm(bank[0][:, 0:COLS], ident_bf[:, :], zeros_bf[:, :], start=True, stop=False)
                    with pe.Fori(0, NBATCH) as b:
                        pe.wait_ge(s_gen_ready, w * NBATCH + b + 1)
                        for t in range(BATCH):
                            last = mm(bank[0][:, 0:COLS], hot_src[:, 0, t], hot_dst[:, 0, t], start=False, stop=False)
                        last.then_inc(s_gen_used, 1)
                    mm(bank[0][:, 0:COLS], ident_bf[:, :], zeros_bf[:, :], start=False, stop=True).then_inc(s_gen_sum, 1)
                    pe.wait_ge(s_gen_at2, w + 1)
                    pe.sem_inc(s_gen_free, 1)

            def degree_rows():
                for i, (a, n) in enumerate(SPANS):
                    for s in range(CH):
                        mm(bank[i][:, 0:n], ones_bf[:, :], at[:, s, a:a + n], start=(s == 0), stop=False)
                    with pe.If(slow != 0):
                        for s in range(CH):
                            mm(bank[i][:, 0:n], ones_bf[:, :], at2[:, s, a:a + n], start=False, stop=False)
                    mm(bank[i][:, 0:COLS], ones_bf[:, :], zeros_bf[:, :], start=False, stop=True).then_inc(s_deg, 1)

            degree_rows()
            pe.wait_ge(s_dinv_row, len(SPANS))
            for c in range(CH):
                last = mm(bank[3][:, c:c + 1], dinv_row[0:1, c * P:(c + 1) * P], one[0:1, 0:1], start=True, stop=True)
            last.then_inc(s_dinvT, 1)

            def neighbours(parts, waits, done):
                for k, lhs in enumerate(parts):
                    for i, (a, n) in enumerate(SPANS):
                        for s in range(CH):
                            waits(k, s)
                            mm(bank[4 + i][:, 0:n], lhs[:, s], at[:, s, a:a + n], start=(k == 0 and s == 0), stop=False)
                        with pe.If(slow != 0):
                            for s in range(CH):
                                mm(bank[4 + i][:, 0:n], lhs[:, s], at2[:, s, a:a + n], start=False, stop=False)
                        for c in range(a // P, (a + n) // P):
                            ends = k == len(parts) - 1 and (c + 1) * P == a + n
                            last = mm(bank[4 + i][:, c * P - a:(c + 1) * P - a], lhs[:, c], ident_bf[:, :], start=False, stop=ends)
                        if k == len(parts) - 1:
                            last.then_inc(done, 1)

            def wait_part1(k, s):
                if k == 0:
                    pe.wait_ge(s_p0, s + 1)
                else:
                    pe.wait_ge(s_p1 if k == 1 else s_p2, 1 if s < HALF else 2)

            neighbours([part[:, 0], part[:, 1], part[:, 2]], wait_part1, s_agg1)
            for i, (a, b) in enumerate(G2_PIECES):
                for c in range(a, b):
                    pe.wait_ge(s_h1t, c // 4 + 1)
                    last = mm(bank[i][:, (c - a) * LAT:(c - a + 1) * LAT], h1t[:, c * P:(c + 1) * P], w2t_sb[:, :], start=True, stop=True)
                last.then_inc(s_h2, 1)

            def wait_part2(k, s):
                if k == 0:
                    pe.wait_ge(s_q1, 1)
                else:
                    pe.wait_ge(s_q2, 1)
                    pe.wait_ge(s_q2_pad, 1)

            neighbours([part2, part3], wait_part2, s_agg2)
            for i, (a, n) in enumerate(SPANS):
                pe.wait_ge(s_zt, i + 1)
                if i >= 1:
                    pe.wait_ge(s_y1, i)
                mm(bank[3][:, 0:n], wd1t_sb[:, :], zt[:, a:a + n], start=True, stop=True).then_inc(s_d1, 1)
                pe.wait_ge(s_y1, i + 1)
                if i == 0:
                    pe.wait_ge(s_agg2s, len(SPANS))
                for k in range(2):
                    if i >= 1:
                        pe.wait_ge(s_y2, 2 * i)
                    mm(bank[k][:, 0:n], wd2t_sb[:, k * P:(k + 1) * P], y1t[:, a:a + n], start=True, stop=True).then_inc(s_d2, 1)
                pe.wait_ge(s_y2, 2 * i + 2)
                for c in range(a // P, (a + n) // P):
                    if c >= 4:
                        pe.wait_ge(s_x2, c - 3)
                    for k in range(2):
                        last = mm(bank[4 + c % 4][:, 0:D], y2t[:, k, c * P:(c + 1) * P], wd3t_sb[:, k], start=(k == 0), stop=(k == 1))
                    last.then_inc(s_d3, 1)
            pe.wait_ge(s_y2, 2 * len(SPANS))
            for c in range(TC):
                pe.wait_ge(s_xn2, c + 1)
                for k in range(KD):
                    last = nc.tensor.transpose(bank[c][:, k * P:(k + 1) * P], xn[:, c % 2, k * P:(k + 1) * P], ident[:, :])
                last.then_inc(s_xn2T, 1)
            pe.wait_ge(s_xn2t, TC)
            pe.wait_ge(s_x2, CH)
            pe.wait_ge(s_ew, 16 * 2 * NE)

            def up(e):
                for m in range(KF):
                    i = KF * e + m
                    if i >= 4:
                        pe.wait_ge(s_gelu, i - 3)
                    for k in range(KD):
                        last = mm(bank[i % 4][:, 0:T], ew1[:, e, k, m * P:(m + 1) * P], xn2t[:, k], start=(k == 0), stop=(k == KD - 1))
                    last.then_inc(s_up, 1)

            up(0)
            for e in range(NE):
                if e + 1 < NE:
                    up(e + 1)
                pe.wait_ge(s_gelu, KF * (e + 1))
                for c in range(TC):
                    i = e * TC + c
                    if i >= 4:
                        pe.wait_ge(s_acc, i - 3)
                    for k in range(KF):
                        last = mm(bank[4 + i % 4][:, 0:D], hidden[:, e % 2, k, c * P:(c + 1) * P], ew2[:, e, k], start=(k == 0), stop=(k == KF - 1))
                    last.then_inc(s_down, 1)


def kernel(x, src, dst, L0_gnn_W1, L0_gnn_b1, L0_gnn_W2, L0_gnn_b2, L0_gnn_Wd1, L0_gnn_bd1, L0_gnn_Wd2,
           L0_gnn_bd2, L0_gnn_Wd3, L0_gnn_bd3, L0_ffn_expert_weights, L0_ffn_expert_indices, L0_ffn_w1,
           L0_ffn_w2):
    import numpy as np
    import concourse.bacc as bacc
    from concourse.bass_utils import run_bass_kernel_spmd

    nc = bacc.Bacc("TRN2", target_bir_lowering=False, num_devices=1)
    given = dict(
        x=x, src=src, dst=dst,
        W1T=np.asarray(L0_gnn_W1).T, b1=L0_gnn_b1, W2T=np.asarray(L0_gnn_W2).T, b2=L0_gnn_b2,
        Wd1T=np.asarray(L0_gnn_Wd1).T, bd1=L0_gnn_bd1,
        Wd2T=np.asarray(L0_gnn_Wd2).T, bd2=np.asarray(L0_gnn_bd2).reshape(-1, P).T,
        Wd3T=np.asarray(L0_gnn_Wd3).T, bd3=L0_gnn_bd3,
        gate_w=L0_ffn_expert_weights, gate_i=L0_ffn_expert_indices, w1=L0_ffn_w1, w2=L0_ffn_w2)
    arrays, args = {}, {}
    for name, a in given.items():
        a = np.ascontiguousarray(a)
        arrays[f"in_{name}"] = a
        args[name] = nc.dram_tensor(f"in_{name}", a.shape, mybir.dt.from_np(a.dtype), kind="ExternalInput").ap()
    out = nc.dram_tensor("out", arrays["in_x"].shape, F32, kind="ExternalOutput").ap()
    gnn_moe(nc, **args, out=out)
    r = run_bass_kernel_spmd(nc, [arrays], core_ids=[0])
    return r.results[0]["out"]
```

```python
from contextlib import ExitStack

import concourse.bass as bass
from concourse import mybir

ALU = mybir.AluOpType
ACT = mybir.ActivationFunctionType
AX = mybir.AxisListType
F32 = mybir.dt.float32
BF16 = mybir.dt.bfloat16
FP16 = mybir.dt.float16
F32R = mybir.dt.float32r
I32 = mybir.dt.int32

P = 128
EPS = 1e-5


def ceil_div(a, b):
    return -(-a // b)


def gnn_moe(nc, x, src, dst, W1T, b1, W2T, b2, Wd1T, bd1, Wd2T, bd2, Wd3T, bd3, gate_w, gate_i,
            w1, w2, out):
    N, D = x.shape
    E = src.shape[0]
    HID, LAT = W1T.shape[1], W2T.shape[1]
    DEC1, DEC2 = Wd1T.shape[1], Wd2T.shape[1]
    T, TOPK = gate_w.shape
    NE, _, FF = w1.shape
    KD, KF = D // P, FF // P
    CH = ceil_div(N, P)
    TAIL = N - (CH - 1) * P
    NP = CH * P
    TC = T // P
    GROUP = 2
    WINDOW = 12
    COLS = CH * WINDOW
    BATCH = 8
    BG = BATCH // GROUP
    ROWT = 4
    ROWG = ROWT // GROUP
    ROWS = ceil_div(E, ROWT * P)
    TILES = ROWS * ROWT
    GROUPS = TILES // GROUP
    NBATCH = ceil_div(TILES, BATCH)
    WIDE = 44
    WIDE_LAST = 2 * WINDOW
    SLOTS = 160
    MORE = SLOTS - P
    J = TC * TOPK
    RING = 4
    BUILD_BANKS = 4
    NWIN = ceil_div(N, WINDOW)
    FULL = E // (ROWT * P)
    LEFT = E - FULL * ROWT * P
    NO_SOURCE = 8191
    FULL_BATCHES = NBATCH - 1
    LAST_GROUPS = GROUPS - FULL_BATCHES * BG
    assert CH * WIDE <= 512 and T % P == 0 and ROWS <= P and N - 1 + WINDOW <= NP and NWIN * WINDOW <= NP
    assert RING == BUILD_BANKS and LEFT > 0 and ROWS == FULL + 1
    FEATURES = 3
    HEAD = 24
    assert (NBATCH - 1 - HEAD) % BUILD_BANKS == 0 and HEAD % BUILD_BANKS == 0 and HEAD > 2 * CH + FEATURES - 1
    SPANS = [(a, min(512, NP - a)) for a in range(0, NP, 512)]
    CHUNKS = [(a // P, (a + n) // P) for a, n in SPANS]
    assert len(SPANS) == 3 and SPANS[0][1] == T

    ctx = ExitStack()
    with ctx:
        def sb(name, shape, dt=F32):
            return ctx.enter_context(nc.sbuf_tensor(name, shape, dt))

        def sb2(name, shape, dt, second):
            with nc.sbuf_tensor(name, shape, dt) as first:
                pass
            size = first.bytes() // P // 4
            return first, sb(second, [P, size], F32R)

        def sem(name):
            return ctx.enter_context(nc.semaphore(name))

        bank = [ctx.enter_context(nc.psum_tensor(f"bank{i}", [P, 512], F32)) for i in range(8)]

        x_sb = sb("x_sb", [P, CH, D])
        w1t_sb = sb("w1t_sb", [P, KD, HID])
        w2t_sb = sb("w2t_sb", [HID, LAT])
        wd1t_sb = sb("wd1t_sb", [2 * LAT, DEC1])
        wd2t_sb = sb("wd2t_sb", [DEC1, DEC2])
        wd3t_sb = sb("wd3t_sb", [P, DEC2 // P, D])
        b1_sb = sb("b1_sb", [HID, 1])
        b2_sb = sb("b2_sb", [2 * LAT, 1])
        bd1_sb = sb("bd1_sb", [DEC1, 1])
        bd2_sb = sb("bd2_sb", [P, DEC2 // P])
        bd3_sb = sb("bd3_sb", [P, D])
        gw_sb = sb("gw_sb", [P, TC, TOPK])
        gi_sb = sb("gi_sb", [P, TC, TOPK], I32)
        ew1, ew1_r = sb2("ew1", [P, NE, KD, FF], F32, "ew1_r")
        ew2, ew2_r = sb2("ew2", [P, NE, KF, D], F32, "ew2_r")

        at, at_r = sb2("at", [P, CH, NP], BF16, "at_r")
        at2, at2_r = sb2("at2", [P, CH, NP], BF16, "at2_r")
        at_flat = at[:, :, :].rearrange("p c n -> p (c n)").bitcast(F32)
        at2_flat = at2[:, :, :].rearrange("p c n -> p (c n)").bitcast(F32)
        rowlen = ROWT * P
        edges = at2_flat[0:ROWS, 0:2 * rowlen].rearrange("p (k e) -> p k e", k=2).bitcast(I32)
        frow = at2_flat[0:ROWS, 2 * rowlen:4 * rowlen].rearrange("p (k e) -> p k e", k=2)
        y1t = at2_flat[:, 0:NP]
        y2t = at2_flat[:, NP:3 * NP].rearrange("p (k n) -> p k n", k=2)
        W_HI = 3
        w1_len, w2_len = KD * FF, KF * D
        w_hi = at_r[:, 0:W_HI * (w1_len + w2_len)].rearrange("p (b n) -> p b n", b=W_HI)
        w_hi_more = at2_r[:, 4 * D:4 * D + w1_len + w2_len]
        hidden = at2_r[:, 0:4 * KF * T].rearrange("p (b h k t) -> p b h k t", b=2, h=2, k=KF)
        w1_lo = ew1_r[:, :].rearrange("p (e k n) -> p e k n", e=NE, k=KD)
        w2_lo = ew2_r[:, :].rearrange("p (e k n) -> p e k n", e=NE, k=KF)

        ring, ring_r = sb2("ring", [P, RING * BATCH * (P + COLS)], BF16, "ring_r")
        n_src = RING * BATCH * P
        hot_src = ring[:, 0:n_src].rearrange("p (r t n) -> p r t n", r=RING, t=BATCH)
        hot_dst = ring[:, n_src:].rearrange("p (r t n) -> p r t n", r=RING, t=BATCH)
        part = ring[:, 0:3 * NP].rearrange("p (k c n) -> p k c n", k=3, c=CH)
        rest = ring[:, 3 * NP:5 * NP].bitcast(F32).rearrange("p (c n) -> p c n", c=CH)
        part2 = ring[:, 0:NP].rearrange("p (c n) -> p c n", c=CH)
        part3 = ring[:, NP:2 * NP].rearrange("p (c n) -> p c n", c=CH)
        rest2 = rest[:, :, 0:LAT]
        H_RAW = 3
        ring_flat = ring[:, :].bitcast(F32)
        xn2t_lo = ring_r[:, 0:KD * T].rearrange("p (k t) -> p k t", k=KD)
        h_raw = ring_flat[:, KD * T:KD * T + H_RAW * T].rearrange("p (b t) -> p b t", b=H_RAW)

        TP = NBATCH * BATCH
        src_lo = sb("src_lo", [P, TP])
        key = sb("key", [P, TP])
        hi_win = sb("hi_win", [P, TP])
        rel = sb("rel", [P, TP])
        isrc = at2_flat[:, 4 * rowlen:4 * rowlen + 3 * TILES].rearrange("p (k t) -> p k t", k=3).bitcast(I32)
        DIFFS = 6
        diff_at = 4 * rowlen + 3 * TILES
        diff = at2_flat[:, diff_at:diff_at + DIFFS * BATCH * P // 2].bitcast(FP16).rearrange(
            "p (r t n) -> p r t n", r=DIFFS, t=BATCH)
        SHARED = [b for b in range(1, NBATCH) if b % 7 != 0]
        carry_key = sb("carry_key", [P, NBATCH])
        hot_carry = sb("hot_carry", [P, NBATCH, CH], BF16)
        gstat = sb("gstat", [P, 4, ROWG])
        gall = sb("gall", [P, 4, GROUPS])
        shift = sb("shift", [P, GROUPS])
        shift_i = sb("shift_i", [1, GROUPS], I32)
        column_i = sb("column_i", [1, NBATCH], I32)
        viol = sb("viol", [P, 5, GROUPS])
        n_viol = sb("n_viol", [P, 8])
        slow_i = sb("slow_i", [1, 1], I32)
        base_t = sb("base_t", [P, 1])

        xnt, xnt_r = sb2("xnt", [P, KD, NP], F32, "xnt_r")
        xnt_flat = xnt[:, :, :].rearrange("p k n -> p (k n)")
        h1t = xnt_flat[:, 0:NP]
        zt = xnt_flat[:, NP:2 * NP]
        xg_t = xnt_r[:, 2 * NP:2 * NP + 4 * KD * SLOTS].rearrange("p (b k h t) -> p b k h t", b=2, h=2, k=KD)
        xn2t = xnt_r[:, 2 * NP:2 * NP + KD * T].rearrange("p (k t) -> p k t", k=KD)
        dinv_row = xnt_flat[:, 2 * NP:3 * NP]
        xn = sb("xn", [P, 2, D])
        SWEPT = 4
        sweep = xn[:, :, :].rearrange("p a n -> p (a n)").bitcast(BF16).rearrange("p (i n) -> p i n", i=SWEPT)
        XG = 3
        xg = ring_flat[:, 0:XG * 2 * D].rearrange("p (b h n) -> p b h n", b=XG, h=2)
        hs_raw = ring_flat[:, XG * 2 * D:XG * 2 * D + KF * SLOTS].rearrange("p (k t) -> p k t", k=KF)
        hs_part = ring_flat[:, XG * 2 * D + KF * SLOTS:XG * 2 * D + 2 * KF * SLOTS].rearrange("p (k t) -> p k t", k=KF)
        hs = at2_r[:, 4 * NP:4 * NP + 4 * KF * SLOTS].rearrange("p (b h k t) -> p b h k t", b=2, h=2, k=KF)
        x2_more = at2_flat[:, 3 * NP:3 * NP + 2 * D].rearrange("p (b n) -> p b n", b=2)
        y_out = at2_flat[:, 0:4 * D].rearrange("p (b h n) -> p b h n", b=2, h=2)
        y_got = at_flat[:, 0:J * D].rearrange("p (j n) -> p j n", j=J)
        rank_hot = ring[:, 5 * NP:5 * NP + J * SLOTS].bitcast(FP16).rearrange("p (j n) -> p j n", j=J)
        skey = xn[:, :, :].rearrange("p a n -> p (a n)")[:, 0:3 * TP].rearrange("p (k t) -> p k t", k=3)

        iota_slots = sb("iota_slots", [P, SLOTS], FP16)
        iota_lanes = iota_slots[:, 0:P]
        before = sb("before", [P, P], BF16)
        token_no = sb("token_no", [P, TC])
        ident = sb("ident", [P, P])
        ident_bf = sb("ident_bf", [P, P], BF16)
        ones_bf = sb("ones_bf", [P, P], BF16)
        zeros_bf = sb("zeros_bf", [P, COLS], BF16)
        one = sb("one", [P, 1])
        eps = sb("eps", [P, 1])

        sums = sb("sums", [P, 2, CH])
        table_use = sb("table_use", [P, 1])
        neg_mean = sb("neg_mean", [P, CH])
        stats = sb("stats", [P, TC, 6])
        mv = sb("mv", [P, TC, 2])
        rstd = sb("rstd", [P, 2, CH])
        h_sb = sb("h_sb", [P, CH, HID])
        dinv_col = sb("dinv_col", [P, CH])
        std_col = sb("std_col", [P, CH])
        gate = sb("gate", [P, TC, NE])
        gate_part = sb("gate_part", [P, 2, TC, NE])
        gif = sb("gif", [P, TC, TOPK])
        expert_no = sb("expert_no", [P, NE])
        chosen = sb("chosen", [P, J + 1, NE], BF16)
        chosen_token = sb("chosen_token", [P, J, NE], FP16)
        ranks = sb("ranks", [P, J, NE])
        rank = sb("rank", [P, J])
        slot_i = sb("slot_i", [P, J], I32)
        load = sb("load", [P, 4])
        path_i = sb("path_i", [1, 2], I32)
        rows_i = sb("rows_i", [P, NE], I32)
        more_i = sb("more_i", [MORE, NE], I32)
        x2_rows = nc.dram_tensor("x2_rows", [T, D], F32).ap()
        y_rows = nc.dram_tensor("y_rows", [NE * SLOTS, D], F32).ap()

        s_edges = sem("s_edges")
        s_edge_pad = sem("s_edge_pad")
        s_x = [sem(f"s_x_chunk{c}") for c in range(CH)]
        s_xpad = sem("s_xpad")
        s_at_zero = sem("s_at_zero")
        s_wg = sem("s_wg")
        s_gates = sem("s_gates")
        s_ew = sem("s_ew")
        s_const = sem("s_const")
        s_dve = sem("s_dve")
        s_rows = sem("s_rows")
        s_rowT = sem("s_rowT")
        s_ready = sem("s_ready")
        s_lo = sem("s_lo")
        s_diff = sem("s_diff")
        s_carry = sem("s_carry")
        s_summed = sem("s_summed")
        s_placed = sem("s_placed")
        s_first = sem("s_first")
        s_slow = sem("s_slow")
        s_sum = sem("s_sum")
        s_mean = sem("s_mean")
        s_square = sem("s_square")
        s_std = sem("s_std")
        s_rstd = sem("s_rstd")
        s_xn = sem("s_xn")
        s_xnT = sem("s_xnT")
        s_xnt = sem("s_xnt")
        s_h = sem("s_h")
        s_hsb = sem("s_hsb")
        s_gen_begin = sem("s_gen_begin")
        s_gen_dve = sem("s_gen_dve")
        s_gen_free = sem("s_gen_free")
        s_gen_ready = sem("s_gen_ready")
        s_gen_used = sem("s_gen_used")
        s_gen_sum = sem("s_gen_sum")
        s_gen_at = sem("s_gen_at")
        s_gen_at2 = sem("s_gen_at2")
        s_deg = sem("s_deg")
        s_deg_std = sem("s_deg_std")
        s_dinv_row = sem("s_dinv_row")
        s_dinvT = sem("s_dinvT")
        s_dinv = sem("s_dinv")
        s_p0 = sem("s_p0")
        s_r0 = sem("s_r0")
        s_p1 = sem("s_p1")
        s_p2 = sem("s_p2")
        s_agg1 = sem("s_agg1")
        s_agg1s = sem("s_agg1s")
        s_h1t = sem("s_h1t")
        s_h2 = sem("s_h2")
        s_g2 = sem("s_g2")
        s_q0 = sem("s_q0")
        s_q0r = sem("s_q0r")
        s_q1 = sem("s_q1")
        s_q2 = sem("s_q2")
        s_q2_pad = sem("s_q2_pad")
        s_agg2 = sem("s_agg2")
        s_agg2s = sem("s_agg2s")
        s_zt = sem("s_zt")
        s_d1 = sem("s_d1")
        s_y1 = sem("s_y1")
        s_d2 = sem("s_d2")
        s_y2 = sem("s_y2")
        s_d3 = sem("s_d3")
        s_x2 = sem("s_x2")
        s_mv2 = sem("s_mv2")
        s_std2 = sem("s_std2")
        s_rstd2 = sem("s_rstd2")
        s_xn2 = sem("s_xn2")
        s_xn2_odd = sem("s_xn2_odd")
        s_xn2T = sem("s_xn2T")
        s_xn2t = sem("s_xn2t")
        s_xn2l = sem("s_xn2l")
        s_whi = sem("s_whi")
        s_wlo = sem("s_wlo")
        s_chosen = sem("s_chosen")
        s_ranks = sem("s_ranks")
        s_route = sem("s_route")
        s_rank_hot = sem("s_rank_hot")
        s_path = sem("s_path")
        s_rows_sum = sem("s_rows_sum")
        s_rows_i = sem("s_rows_i")
        s_x2_stored = sem("s_x2_stored")
        s_gathered = [sem(f"s_gathered{i}") for i in range(3)]
        s_xgT = sem("s_xgT")
        s_xg_hi = sem("s_xg_hi")
        s_xg_lo = sem("s_xg_lo")
        s_whi_act = sem("s_whi_act")
        s_up_sp = sem("s_up_sp")
        s_hs_part = sem("s_hs_part")
        s_hs_sum = sem("s_hs_sum")
        s_gelu_sp = sem("s_gelu_sp")
        s_hs_hi = sem("s_hs_hi")
        s_hs_lo = sem("s_hs_lo")
        s_down_sp = sem("s_down_sp")
        s_y = sem("s_y")
        s_y_more = sem("s_y_more")
        s_y_stored = [sem(f"s_y_stored{i}") for i in range(2)]
        s_y_got = [sem(f"s_y_got{c}") for c in range(TC)]
        s_first_choice = sem("s_first_choice")
        s_done = sem("s_done")
        s_up = sem("s_up")
        s_gelu = sem("s_gelu")
        s_hhi = sem("s_hhi")
        s_hlo = sem("s_hlo")
        s_down = sem("s_down")
        s_acc = sem("s_acc")
        s_out = sem("s_out")
        s_out_rest = sem("s_out_rest")

        block = ctx.enter_context(nc.Block())
        NCONST = 14
        PAD_ROW = (ROWS - 1) // 32 * 32
        NWG = 11
        HALF = ceil_div(CH, 2)
        HALVES = [(0, HALF), (HALF, CH)]
        WARM = 40
        H2_BANK = [3, 7, 3]
        D1_BANK = [3, 2, 3]

        def is_slow(eng):
            eng.wait_ge(s_slow, 1)
            _, (v,) = nc.values_load_multi_w_load_instructions(
                slow_i[0:1, 0:1], engines=[eng.engine], min_val=0, max_val=1,
                skip_runtime_bounds_check_because="the flag is clamped to 0 and 1 when it is made")
            return v

        def is_path(eng, which):
            eng.wait_ge(s_path, 2)
            _, (v,) = nc.values_load_multi_w_load_instructions(
                path_i[0:1, which:which + 1], engines=[eng.engine], min_val=0, max_val=1,
                skip_runtime_bounds_check_because="the flag is 0 or 1")
            return v

        def weights(e):
            return [ew1[:, e].rearrange("p k n -> p (k n)"), ew2[:, e].rearrange("p k n -> p (k n)")]

        def weights_lo(e):
            return [ew1_r[:, e * w1_len:(e + 1) * w1_len], ew2_r[:, e * w2_len:(e + 1) * w2_len]]

        def weights_hi(e, slots=W_HI):
            place = w_hi[:, e % slots] if e % slots < W_HI else w_hi_more
            return [place[:, 0:w1_len], place[:, w1_len:]]

        def normal(c):
            return xn[:, c] if c < 2 else x2_more[:, c - 2]

        def load_edges(eng, k, a):
            eng.dma_start(edges[0:FULL, k, :],
                          a[0:FULL * rowlen].rearrange("(r e) -> r e", e=rowlen)).then_inc(s_edges, 16)
            eng.dma_start(edges[FULL:ROWS, k, 0:LEFT],
                          a[FULL * rowlen:E].rearrange("(a e) -> a e", a=1)).then_inc(s_edges, 16)

        @block.sync
        def _(sp):
            sp.wait_ge(s_edge_pad, 2)
            load_edges(sp, 0, src)
            for c in range(CH):
                n = P if c < CH - 1 else TAIL
                if n < P:
                    sp.wait_ge(s_xpad, 1)
                sp.dma_start(x_sb[0:n, c, :], x[c * P:c * P + n, :]).then_inc(s_x[c], 16)
            sp.dma_start(w1t_sb[:, :, :], W1T.rearrange("(k p) n -> p k n", p=P)).then_inc(s_wg, 16)
            sp.dma_start(w2t_sb[:, :], W2T).then_inc(s_wg, 16)
            for k in range(2):
                sp.dma_start(wd1t_sb[k * LAT:(k + 1) * LAT, :], Wd1T).then_inc(s_wg, 16)
            sp.dma_start(wd2t_sb[:, :], Wd2T).then_inc(s_wg, 16)
            sp.dma_start(wd3t_sb[:, :, :], Wd3T.rearrange("(k p) n -> p k n", p=P)).then_inc(s_wg, 16)
            sp.dma_start(b1_sb[:, :], b1.rearrange("(p a) -> p a", a=1)).then_inc(s_wg, 16)
            sp.dma_start(bd1_sb[:, :], bd1.rearrange("(p a) -> p a", a=1)).then_inc(s_wg, 16)
            sp.dma_start(bd2_sb[:, :], bd2).then_inc(s_wg, 16)
            sp.dma_start(bd3_sb[:, :], bd3.rearrange("(a n) -> a n", a=1).to_broadcast([P, D])).then_inc(s_wg, 16)
            sp.wait_ge(s_const, NCONST)
            sp.dma_start(b2_sb[0:LAT, :], b2.rearrange("(p a) -> p a", a=1)).then_inc(s_wg, 16)
            sp.dma_start(gw_sb[:, :, :], gate_w.rearrange("(c p) k -> p c k", p=P)).then_inc(s_gates, 16)
            sp.dma_start(gi_sb[:, :, :], gate_i.rearrange("(c p) k -> p c k", p=P)).then_inc(s_gates, 16)
            for e in range(NE):
                sp.dma_start(ew1[:, e], w1[e].rearrange("(k p) n -> p k n", p=P)).then_inc(s_ew, 16)
                sp.dma_start(ew2[:, e], w2[e].rearrange("(k p) n -> p k n", p=P)).then_inc(s_ew, 16)
            def store_rest():
                for c in range(TC, CH):
                    n = P if c < CH - 1 else TAIL
                    sp.wait_ge(s_x2, c + 1)
                    sp.dma_start(out[c * P:c * P + n, :], x_sb[0:n, c, :]).then_inc(s_out_rest, 16)

            dense = is_path(sp, 0)
            with sp.If(dense != 0):
                store_rest()
                for c in range(TC):
                    sp.wait_ge(s_acc, TC * (NE - 1) + c + 1)
                    sp.dma_start(out[c * P:(c + 1) * P, :], x_sb[:, c, :]).then_inc(s_out, 16)
                sp.wait_ge(s_out_rest, 16 * (CH - TC))
                sp.wait_ge(s_out, 16 * TC)
            sparse = is_path(sp, 1)
            with sp.If(sparse != 0):
                for i, rows in enumerate((xn, x2_more)):
                    sp.wait_ge(s_xn2, i + 1)
                    sp.wait_ge(s_xn2_odd, i + 1)
                    sp.dma_start(x2_rows[2 * i * P:2 * (i + 1) * P, :].rearrange("(c p) n -> p c n", p=P),
                                 rows[:, :, :]).then_inc(s_x2_stored, 16)
                for e in range(NE):
                    if e == 2:
                        store_rest()
                    r = e * SLOTS
                    sp.wait_ge(s_y, e + 1)
                    sp.dma_start(y_rows[r:r + P, :], y_out[:, e % 2, 0]).then_inc(s_y_stored[e % 2], 16)
                    sp.wait_ge(s_y_more, e + 1)
                    sp.dma_start(y_rows[r + P:r + SLOTS, :], y_out[0:MORE, e % 2, 1]).then_inc(s_y_stored[e % 2], 16)
                for c in range(TC):
                    sp.wait_ge(s_done, c + 1)
                    sp.dma_start(out[c * P:(c + 1) * P, :], x_sb[:, c, :]).then_inc(s_out, 16)
                sp.wait_ge(s_out_rest, 16 * (CH - TC))
                sp.wait_ge(s_out, 16 * TC)

        @block.gpsimd
        def _(pool):
            nc.gpsimd.memset(ident[:, :], 0.0).then_inc(s_const, 1)
            nc.gpsimd.memset(ident_bf[:, :], 0.0).then_inc(s_const, 1)
            pool.wait_ge(s_const, 2)
            for m in (ident, ident_bf):
                nc.gpsimd.affine_select(out=m[:, :], in_=m[:, :], compare_op=ALU.not_equal, fill=1.0, base=0,
                                        pattern=[[-1, P]], channel_multiplier=1).then_inc(s_const, 1)
            nc.gpsimd.iota(iota_slots[:, :], pattern=[[1, SLOTS]], base=0, channel_multiplier=0,
                           allow_small_or_imprecise_dtypes=True).then_inc(s_const, 1)
            nc.gpsimd.iota(expert_no[:, :], pattern=[[1, NE]], base=0, channel_multiplier=0,
                           allow_small_or_imprecise_dtypes=True).then_inc(s_const, 1)
            nc.gpsimd.memset(eps[:, :], EPS).then_inc(s_const, 1)
            nc.gpsimd.memset(one[:, :], 1.0).then_inc(s_const, 1)
            nc.gpsimd.memset(ones_bf[:, :], 1.0).then_inc(s_const, 1)
            nc.gpsimd.iota(token_no[:, :], pattern=[[P, TC]], base=0, channel_multiplier=1,
                           allow_small_or_imprecise_dtypes=True).then_inc(s_const, 1)
            nc.gpsimd.memset(chosen[:, J], 0.0).then_inc(s_const, 1)
            pool.wait_ge(s_const, 11)
            nc.gpsimd.affine_select(out=before[:, :], in_=ones_bf[:, :], compare_op=ALU.is_gt, fill=0.0, base=0,
                                    pattern=[[1, P]], channel_multiplier=-1).then_inc(s_const, 1)
            nc.gpsimd.memset(b2_sb[:, :], 0.0).then_inc(s_const, 1)
            nc.gpsimd.memset(zeros_bf[:, :], 0.0).then_inc(s_const, 1)
            nc.gpsimd.memset(x_sb[:, CH - 1, :], 0.0).then_inc(s_xpad, 1)
            nc.gpsimd.memset(at_flat, 0.0).then_inc(s_at_zero, 1)
            pool.wait_ge(s_lo, 1)
            for i, b in enumerate(SHARED):
                if i >= DIFFS:
                    pool.wait_ge(s_ready, SHARED[i - DIFFS] + 1)
                nc.gpsimd.tensor_tensor(diff[:, i % DIFFS], iota_lanes[:, :].unsqueeze(1).to_broadcast([P, BATCH, P]),
                                        src_lo[:, b * BATCH:(b + 1) * BATCH].unsqueeze(2).to_broadcast([P, BATCH, P]),
                                        ALU.subtract).then_inc(s_diff, 1)
            pool.wait_ge(s_agg1, len(SPANS))
            nc.gpsimd.memset(part3[:, :, LAT:], 0.0).then_inc(s_q2_pad, 1)
            dense, sparse = is_path(pool, 0), is_path(pool, 1)
            pool.wait_ge(s_ew, 16 * 2 * NE)
            pool.wait_ge(s_agg2, len(SPANS))
            for e in range(2):
                for w, hi in zip(weights(e), weights_hi(e)):
                    nc.gpsimd.tensor_copy(hi, w).then_inc(s_whi, 1)
            with pool.If(sparse != 0):
                def gather(e):
                    if e >= XG:
                        pool.wait_ge(s_xgT, 2 * (e - XG + 1))
                    nc.gpsimd.indirect_dma_start(xg[:, e % XG, 0], None, x2_rows,
                                                 bass.IndirectOffsetOnAxis(rows_i[:, e:e + 1].bitcast(mybir.dt.uint32), 0)
                                                 ).then_inc(s_gathered[e % XG], 16)
                    nc.gpsimd.indirect_dma_start(xg[0:MORE, e % XG, 1], None, x2_rows,
                                                 bass.IndirectOffsetOnAxis(more_i[:, e:e + 1].bitcast(mybir.dt.uint32), 0)
                                                 ).then_inc(s_gathered[e % XG], 16)

                pool.wait_ge(s_rows_i, 2)
                pool.wait_ge(s_x2_stored, 16 * 2)
                for e in range(NE):
                    gather(e)
                for i in range(2):
                    pool.wait_ge(s_y_stored[i], 32 * NE // 2)
                for j in range(J):
                    nc.gpsimd.indirect_dma_start(y_got[:, j], None, y_rows,
                                                 bass.IndirectOffsetOnAxis(slot_i[:, j:j + 1].bitcast(mybir.dt.uint32), 0)
                                                 ).then_inc(s_y_got[j // TOPK], 16)
            with pool.If(dense != 0):
                for e in range(2, NE):
                    if e >= W_HI:
                        pool.wait_ge(s_down, TC * (e - W_HI + 1))
                    for w, hi in zip(weights(e), weights_hi(e)):
                        nc.gpsimd.tensor_copy(hi, w).then_inc(s_whi, 1)

        @block.vector
        def _(dve):
            chain = [0]

            def link(ins):
                chain[0] += 1
                ins.then_inc(s_dve, 1)
                dve.wait_ge(s_dve, chain[0])

            v = nc.vector
            v.memset(edges[PAD_ROW:ROWS, 0, LEFT:], NO_SOURCE).then_inc(s_edge_pad, 1)
            v.memset(edges[PAD_ROW:ROWS, 1, LEFT:], N).then_inc(s_edge_pad, 1)
            dve.wait_ge(s_edges, 64)
            glen = GROUP * P
            i_dst = edges[:, 1, :].rearrange("p (h e) -> p h e", h=ROWG)
            v.tensor_copy(frow[:, 0, :], edges[:, 0, :])
            link(v.tensor_reduce(gstat[0:ROWS, 0], i_dst, AX.X, ALU.min))
            for h in range(ROWG):
                last = v.tensor_scalar(frow[:, 1, h * glen:(h + 1) * glen], edges[:, 1, h * glen:(h + 1) * glen],
                                       gstat[0:ROWS, 0, h:h + 1], None, ALU.subtract)
            v.tensor_reduce(gstat[0:ROWS, 1], i_dst, AX.X, ALU.max)
            v.tensor_reduce(gstat[0:ROWS, 2], i_dst[:, :, 0:glen - P], AX.X, ALU.max)
            v.tensor_reduce(gstat[0:ROWS, 3], i_dst[:, :, glen - P:glen], AX.X, ALU.min).then_inc(s_rows, 1)
            v.memset(key[:, TILES:TP], -1.0)
            v.memset(src_lo[:, TILES:TP], 0.0)
            link(v.memset(hi_win[:, TILES:TP], 0.0))

            dve.wait_ge(s_rowT, 1)

            def by_tile(bank_, width=TILES):
                return bank_[:, 0:width].rearrange("p (t r) -> p r t", t=ROWT)

            v.tensor_copy(gall[:, 0:3], bank[2][:, 0:3 * GROUPS].rearrange("p (k g) -> p k g", k=3))
            v.tensor_copy(rel[:, 0:TILES].rearrange("p (r t) -> p r t", t=ROWT), by_tile(bank[1]))
            link(v.tensor_copy(isrc[:, 0, :].rearrange("p (r t) -> p r t", t=ROWT), by_tile(bank[0])))
            v.tensor_scalar(isrc[:, 1], isrc[:, 0], P - 1, None, ALU.bitwise_and)
            link(v.tensor_scalar(isrc[:, 2], isrc[:, 0], 7, None, ALU.arith_shift_right))
            v.tensor_copy(src_lo[:, 0:TILES], isrc[:, 1]).then_inc(s_lo, 1)
            link(v.tensor_scalar(hi_win[:, 0:TILES], isrc[:, 2], float(WINDOW), None, ALU.mult))
            v.tensor_tensor(viol[:, 0, 0:GROUPS - 1], gall[:, 0, 1:GROUPS], gall[:, 0, 0:GROUPS - 1], ALU.subtract)
            pieces = [(0, FULL_BATCHES, BG, WIDE), (FULL_BATCHES * BG, 1, LAST_GROUPS, WIDE_LAST)]
            for a, nb, ng, wide in pieces:
                of_batch = gall[:, 0, a:a + (nb - 1) * BG + 1:BG]
                last = v.tensor_tensor(shift[:, a:a + nb * ng].rearrange("p (b g) -> p b g", g=ng),
                                       gall[:, 0, a:a + nb * ng].rearrange("p (b g) -> p b g", g=ng),
                                       of_batch.unsqueeze(2).to_broadcast([P, nb, ng]), ALU.subtract)
                v.tensor_scalar(column_i[:, a // BG:a // BG + nb], of_batch[0:1], float(NP - wide), None,
                                ALU.min).then_inc(s_first, 1)
            link(last)
            for a, nb, ng, wide in pieces:
                v.tensor_scalar(shift_i[:, a:a + nb * ng], shift[0:1, a:a + nb * ng], float(wide - WINDOW), 0.0,
                                ALU.min, ALU.max).then_inc(s_first, 1)
            link(v.tensor_tensor(key[:, 0:TILES], hi_win[:, 0:TILES], rel[:, 0:TILES], ALU.add))

            def one_hots(slot, lo, hi, lanes, i_diff=None):
                n = BATCH
                if i_diff is None:
                    v.tensor_tensor(hot_src[:, slot], iota_lanes[:, :].unsqueeze(1).to_broadcast([P, n, P]),
                                    lo.unsqueeze(2).to_broadcast([P, n, P]), ALU.is_equal)
                else:
                    dve.wait_ge(s_diff, i_diff + 1)
                    v.tensor_scalar(hot_src[:, slot], diff[:, i_diff % DIFFS], 0.0, None, ALU.is_equal)
                return v.tensor_tensor(hot_dst[:, slot], lanes.unsqueeze(1).to_broadcast([P, n, COLS]),
                                       hi.unsqueeze(2).to_broadcast([P, n, COLS]), ALU.is_equal)

            dve.wait_ge(s_sum, CH)
            v.tensor_scalar(neg_mean[:, :], sums[:, 0], -1.0 / D, None, ALU.mult).then_inc(s_mean, 1)
            dve.wait_ge(s_const, NCONST)
            for b in range(NBATCH):
                if b >= RING - 1:
                    dve.wait_ge(s_summed, b - RING + 2)
                t0 = b * BATCH
                one_hots(b % RING, src_lo[:, t0:t0 + BATCH], key[:, t0:t0 + BATCH],
                         iota_lanes[:, 0:COLS], SHARED.index(b) if b in SHARED else None).then_inc(s_ready, 1)
                if b == 0:
                    n = FULL_BATCHES
                    link(v.tensor_tensor(viol[:, 1, 0:n], rel[:, BATCH - 1:n * BATCH:BATCH], viol[:, 0, BG - 1:n * BG:BG],
                                         ALU.is_equal))
                    link(v.scalar_tensor_tensor(carry_key[:, 0:n], hi_win[:, BATCH - 1:n * BATCH:BATCH],
                                                1.0, viol[:, 1, 0:n], ALU.add, ALU.mult))
                    v.tensor_tensor(hot_carry[:, 0:n],
                                    iota_lanes[:, 1:COLS + 1:WINDOW].unsqueeze(1).to_broadcast([P, n, CH]),
                                    carry_key[:, 0:n].unsqueeze(2).to_broadcast([P, n, CH]),
                                    ALU.is_equal).then_inc(s_carry, 1)
                if b == FEATURES:
                    dve.wait_ge(s_std, 1)
                    dve.wait_ge(s_mean, 1)
                    link(v.reciprocal(rstd[:, 0], rstd[:, 1]))
                    v.tensor_tensor(rstd[:, 1], neg_mean[:, :], rstd[:, 0], ALU.mult).then_inc(s_rstd, 1)
                if b == 2:
                    dve.wait_ge(s_carry, 1)
                    v.tensor_copy(gall[:, 3], bank[3][:, 0:GROUPS])
                    link(v.memset(viol[:, 1:4, GROUPS - 1:GROUPS], 0.0))
                    link(v.tensor_tensor(viol[:, 0], gall[:, 1], gall[:, 0], ALU.subtract))
                    link(v.tensor_scalar(viol[:, 0], viol[:, 0], float(WINDOW) - 0.5, None, ALU.is_gt))
                    for a, nb, ng, wide in pieces:
                        link(v.tensor_scalar(viol[:, 4, a:a + nb * ng], shift[:, a:a + nb * ng], float(wide - WINDOW), None,
                                             ALU.is_gt))
                        of_batch = gall[:, 0, a:a + (nb - 1) * BG + 1:BG]
                        at_first = viol[:, 4, a:a + (nb - 1) * BG + 1:BG]
                        link(v.scalar_tensor_tensor(at_first, of_batch, float(NP - wide), at_first, ALU.is_gt, ALU.max))
                    v.tensor_tensor(viol[:, 1, 0:GROUPS - 1], gall[:, 1, 0:GROUPS - 1], gall[:, 0, 1:GROUPS], ALU.is_gt)
                    v.tensor_tensor(viol[:, 2, 0:GROUPS - 1], gall[:, 2, 0:GROUPS - 1], gall[:, 0, 1:GROUPS], ALU.is_ge)
                    link(v.tensor_tensor(viol[:, 3], gall[:, 3], gall[:, 0], ALU.is_le))
                    link(v.tensor_reduce(n_viol[:, 0:1], viol[:, :, :].rearrange("p a b -> p (a b)"), AX.X, ALU.max))
                    v.tensor_copy(slow_i[:, :], n_viol[0:1, 0:1]).then_inc(s_slow, 1)

            slow = is_slow(dve)
            with dve.If(slow != 0):
                dve.wait_ge(s_summed, NBATCH)
                dve.wait_ge(s_placed, NBATCH)
                v.memset(at2_flat, 0.0).then_inc(s_gen_begin, 1)
                v.memset(base_t[:, :], 0.0)
                v.memset(skey[:, 0, TILES:TP], -float(2 * NP))
                v.tensor_tensor(skey[:, 0, 0:TILES].rearrange("p (g t) -> p g t", t=GROUP),
                                rel[:, 0:TILES].rearrange("p (g t) -> p g t", t=GROUP),
                                gall[:, 0].unsqueeze(2).to_broadcast([P, GROUPS, GROUP]), ALU.add).then_inc(s_gen_begin, 1)
                dve.wait_ge(s_gen_begin, 2)
                steps = 6
                with dve.Fori(0, NWIN) as w:
                    turn = [0]

                    def again(ins):
                        turn[0] += 1
                        ins.then_inc(s_gen_dve, 1)
                        dve.wait_ge(s_gen_dve, w * steps + turn[0])

                    again(v.tensor_scalar(skey[:, 1], skey[:, 0], base_t[:, :], None, ALU.subtract))
                    again(v.tensor_scalar(skey[:, 2], skey[:, 1], float(WINDOW), None, ALU.is_lt))
                    again(v.scalar_tensor_tensor(skey[:, 2], skey[:, 1], 0.0, skey[:, 2], ALU.is_ge, ALU.mult))
                    again(v.scalar_tensor_tensor(skey[:, 1], skey[:, 1], 1.0, hi_win[:, :], ALU.add, ALU.add))
                    again(v.tensor_tensor(skey[:, 1], skey[:, 1], skey[:, 2], ALU.mult))
                    v.tensor_scalar(base_t[:, :], base_t[:, :], float(WINDOW), None, ALU.add).then_inc(s_gen_dve, 1)
                    with dve.Fori(0, NBATCH) as b:
                        dve.wait_ge(s_gen_dve, w * steps + steps)
                        dve.wait_ge(s_gen_used, w * NBATCH + b + 1)
                        one_hots(0, src_lo[:, bass.ds(b * BATCH, BATCH)], skey[:, 1, bass.ds(b * BATCH, BATCH)],
                                 iota_lanes[:, 1:COLS + 1]).then_inc(s_gen_ready, 1)
                    dve.wait_ge(s_gen_at, w + 1)
                    v.tensor_tensor(at2[:, :, bass.ds(w * WINDOW, WINDOW)], bank[0][:, 0:COLS].rearrange("p (c n) -> p c n", c=CH),
                                    at[:, :, bass.ds(w * WINDOW, WINDOW)], ALU.subtract).then_inc(s_gen_at2, 1)
                dve.wait_ge(s_gen_at2, NWIN)

            dve.wait_ge(s_deg_std, 1)
            v.reciprocal(dinv_col[:, :], std_col[:, :]).then_inc(s_dinv, 1)
            dve.wait_ge(s_dinv, 1)
            for i, (a, b) in enumerate(HALVES):
                for c in range(a, b):
                    dve.wait_ge(s_p0, c + 1)
                    last = v.scalar_tensor_tensor(rest[:, c], h_sb[:, c], dinv_col[:, c:c + 1], part[:, 0, c],
                                                  ALU.mult, ALU.subtract)
                last.then_inc(s_r0, 1)
            for i, (a, b) in enumerate(HALVES):
                dve.wait_ge(s_p1, i + 1)
                v.tensor_tensor(part[:, 2, a:b], rest[:, a:b], part[:, 1, a:b], ALU.subtract).then_inc(s_p2, 1)

            dve.wait_ge(s_gates, 32)
            link(v.tensor_copy(gif[:, :, :], gi_sb[:, :, :]))
            gif_j = gif[:, :, :].rearrange("p c k -> p (c k)")
            v.tensor_tensor(chosen[:, 0:J], expert_no[:, :].unsqueeze(1).to_broadcast([P, J, NE]),
                            gif_j.unsqueeze(2).to_broadcast([P, J, NE]), ALU.is_equal).then_inc(s_chosen, 1)
            dve.wait_ge(s_wg, 16 * NWG)
            for c in range(CH):
                last = v.tensor_tensor(x_sb[:, c], x_sb[:, c], bd3_sb[:, :], ALU.add)
            link(last)
            for c in range(TC):
                for k in range(TOPK):
                    last = v.tensor_scalar(gate_part[:, k, c], expert_no[:, :], gif[:, c, k:k + 1], gw_sb[:, c, k:k + 1],
                                           ALU.is_equal, ALU.mult)
            link(last)
            link(v.tensor_tensor(gate[:, :, :], gate_part[:, 0], gate_part[:, 1], ALU.add))
            routed = [0]

            def route(ins):
                routed[0] += 1
                ins.then_inc(s_route, 1)
                dve.wait_ge(s_route, routed[0])

            dve.wait_ge(s_chosen, 1)
            dve.wait_ge(s_ranks, 1)
            v.tensor_tensor(chosen_token[:, :, :].rearrange("p (c k) e -> p c (k e)", k=TOPK),
                            chosen[:, 0:J].rearrange("p (c k) e -> p c (k e)", k=TOPK),
                            token_no[:, :].unsqueeze(2).to_broadcast([P, TC, TOPK * NE]), ALU.mult).then_inc(s_rank_hot, 1)
            v.tensor_reduce(load[:, 0:1], bank[7][:, J * NE:(J + 1) * NE], AX.X, ALU.max)
            v.tensor_reduce(load[:, 1:2], bank[7][:, J * NE:(J + 1) * NE], AX.X, ALU.add)
            route(v.tensor_tensor(ranks[:, :, :], chosen[:, 0:J], bank[7][:, 0:J * NE].rearrange("p (j e) -> p j e", e=NE),
                                  ALU.mult))
            route(v.tensor_reduce(rank[:, :], ranks[:, :, :], AX.X, ALU.add))
            for j in range(J):
                v.tensor_scalar(rank_hot[:, j], iota_slots[:, :], rank[:, j:j + 1], None, ALU.is_equal).then_inc(s_rank_hot, 1)
            v.scalar_tensor_tensor(slot_i[:, :], gif_j, float(SLOTS), rank[:, :], ALU.mult, ALU.add)
            v.tensor_scalar(load[:, 2:3], load[:, 0:1], float(SLOTS), None, ALU.is_gt)
            route(v.tensor_scalar(load[:, 3:4], load[:, 1:2], float(T * TOPK), None, ALU.is_lt))
            v.tensor_tensor(path_i[:, 0:1], load[0:1, 2:3], load[0:1, 3:4], ALU.max).then_inc(s_path, 1)
            route(v.tensor_tensor(load[:, 0:1], load[:, 2:3], load[:, 3:4], ALU.max))
            v.tensor_scalar(path_i[:, 1:2], load[0:1, 0:1], 0.0, None, ALU.is_equal).then_inc(s_path, 1)

            g2 = h_sb[:, :, 0:LAT]

            def scale_sum1(i):
                a, n = SPANS[i]
                dve.wait_ge(s_dinv_row, i + 1)
                dve.wait_ge(s_agg1, i + 1)
                v.tensor_tensor(h1t[:, a:a + n], bank[4 + i][:, 0:n], dinv_row[:, a:a + n], ALU.mult).then_inc(s_agg1s, 1)

            def scale_h2(i):
                a, b = CHUNKS[i]
                dve.wait_ge(s_h2, i + 1)
                v.tensor_tensor(g2[:, a:b], bank[H2_BANK[i]][:, 0:(b - a) * LAT].rearrange("p (c n) -> p c n", n=LAT),
                                dinv_col[:, a:b].unsqueeze(2).to_broadcast([P, b - a, LAT]), ALU.mult).then_inc(s_g2, 1)

            def rest_h2(i):
                a, b = CHUNKS[i]
                dve.wait_ge(s_g2, i + 1)
                dve.wait_ge(s_q0, i + 1)
                v.tensor_tensor(rest2[:, a:b], g2[:, a:b], part2[:, a:b, 0:LAT], ALU.subtract).then_inc(s_q0r, 1)

            def third_h2(i):
                a, b = CHUNKS[i]
                dve.wait_ge(s_q0r, i + 1)
                dve.wait_ge(s_q1, i + 1)
                v.tensor_tensor(part3[:, a:b, 0:LAT], rest2[:, a:b], part2[:, a:b, LAT:2 * LAT], ALU.subtract).then_inc(s_q2, 1)

            scale_sum1(0)
            scale_sum1(1)
            scale_h2(0)
            scale_sum1(2)
            rest_h2(0)
            scale_h2(1)
            third_h2(0)
            scale_h2(2)
            rest_h2(1)
            rest_h2(2)
            third_h2(1)
            third_h2(2)
            dve.wait_ge(s_rows_sum, 1)
            v.tensor_copy(rows_i[:, :], bank[0][:, 0:NE]).then_inc(s_rows_i, 1)
            v.tensor_copy(more_i[:, :], bank[0][0:MORE, NE:2 * NE]).then_inc(s_rows_i, 1)
            dense, sparse = is_path(dve, 0), is_path(dve, 1)
            for i, (a, n) in enumerate(SPANS):
                dve.wait_ge(s_agg2, i + 1)
                v.tensor_tensor(zt[:, a:a + n], bank[4 + i][:, 0:n], dinv_row[:, a:a + n], ALU.mult).then_inc(s_agg2s, 1)

            def weights_rest(e):
                dve.wait_ge(s_whi, 2 * (e + 1))
                second_parts(e)

            def second_parts(e, slots=W_HI, only=None):
                for i, (w, hi, lo) in enumerate(zip(weights(e), weights_hi(e, slots), weights_lo(e))):
                    if only is not None and i != only:
                        continue
                    v.tensor_tensor(lo, w, hi.bitcast(F32), ALU.subtract).then_inc(s_wlo, 1)

            def hidden_rest(i):
                e, k = divmod(i, KF)
                dve.wait_ge(s_hhi, i + 1)
                v.tensor_tensor(hidden[:, e % 2, 1, k], h_raw[:, i % H_RAW], hidden[:, e % 2, 0, k].bitcast(F32),
                                ALU.subtract).then_inc(s_hlo, 1)

            def tokens_rest(c):
                dve.wait_ge(s_xn2t, c + 1)
                v.tensor_tensor(xn2t_lo[:, :, c * P:(c + 1) * P], bank[2 + c % 2][:, :].rearrange("p (k n) -> p k n", k=KD),
                                xn2t[:, :, c * P:(c + 1) * P].bitcast(F32), ALU.subtract).then_inc(s_xn2l, 1)

            for c in range(CH):
                dve.wait_ge(s_d3, c + 1)
                v.tensor_tensor(x_sb[:, c], x_sb[:, c], bank[4 + c % 4][:, 0:D], ALU.add).then_inc(s_x2, 1)
                if c < TC:
                    dve.wait_ge(s_x2, c + 1)
                    link(v.bn_stats(stats[:, c], x_sb[:, c]))
                    ins = v.bn_aggr(mv[:, c], stats[:, c])
                    if c == TC - 1:
                        ins.then_inc(s_mv2, 1)
                        dve.wait_ge(s_mv2, 1)
                        dve.wait_ge(s_std2, 1)
                        link(v.reciprocal(rstd[:, 0, 0:TC], rstd[:, 1, 0:TC]))
                        v.scalar_tensor_tensor(rstd[:, 1, 0:TC], mv[:, 0:TC, 0], -1.0, rstd[:, 0, 0:TC],
                                               ALU.mult, ALU.mult).then_inc(s_rstd2, 1)
                        dve.wait_ge(s_rstd2, 1)
                        for t in range(1, TC, 2):
                            v.tensor_scalar(normal(t), x_sb[:, t], rstd[:, 0, t:t + 1], rstd[:, 1, t:t + 1], ALU.mult,
                                            ALU.add).then_inc(s_xn2_odd, 1)
                if c == TC + 1:
                    weights_rest(0)
            weights_rest(1)
            with dve.If(sparse != 0):
                def gathered_rest(e):
                    for i in range(2):
                        dve.wait_ge(s_xg_hi, 2 * e + i + 1)
                        v.tensor_tensor(xg_t[:, e % 2, 2 * i:2 * i + 2, 1],
                                        bank[i][:, 0:2 * SLOTS].rearrange("p (k t) -> p k t", k=2),
                                        xg_t[:, e % 2, 2 * i:2 * i + 2, 0].bitcast(F32), ALU.subtract).then_inc(s_xg_lo, 1)

                def sum_hidden(e):
                    if e >= 1:
                        dve.wait_ge(s_hs_hi, e)
                        dve.wait_ge(s_hs_lo, e)
                    for m in range(KF):
                        dve.wait_ge(s_hs_part, KF * e + m + 1)
                        v.tensor_tensor(hs_raw[:, m], bank[2 + m][:, 0:SLOTS], hs_part[:, m],
                                        ALU.add).then_inc(s_hs_sum, 1)

                def keep_results(e):
                    dve.wait_ge(s_down_sp, 2 * e + 1)
                    if e >= 2:
                        dve.wait_ge(s_y_stored[e % 2], 32 * (e // 2))
                    v.tensor_copy(y_out[:, e % 2, 0], bank[4 + 2 * (e % 2)][:, 0:D]).then_inc(s_y, 1)

                gathered_rest(0)
                gathered_rest(1)
                sum_hidden(0)
                for e in range(NE):
                    if e + 2 < NE:
                        dve.wait_ge(s_whi_act, 2 * (e + 1))
                        second_parts(e + 2, W_HI + 1, 0)
                    dve.wait_ge(s_hs_hi, e + 1)
                    v.tensor_tensor(hs[:, e % 2, 1], hs_raw, hs[:, e % 2, 0].bitcast(F32), ALU.subtract).then_inc(s_hs_lo, 1)
                    if e >= 1:
                        keep_results(e - 1)
                    if e + 2 < NE:
                        second_parts(e + 2, W_HI + 1, 1)
                        gathered_rest(e + 2)
                    if e + 1 < NE:
                        sum_hidden(e + 1)
                keep_results(NE - 1)
                for c in range(TC):
                    dve.wait_ge(s_y_got[c], 16 * TOPK)
                    v.scalar_tensor_tensor(x_sb[:, c], y_got[:, TOPK * c], gw_sb[:, c, 0:1], x_sb[:, c],
                                           ALU.mult, ALU.add).then_inc(s_first_choice, 1)
                    dve.wait_ge(s_first_choice, c + 1)
                    v.scalar_tensor_tensor(x_sb[:, c], y_got[:, TOPK * c + 1], gw_sb[:, c, 1:2], x_sb[:, c],
                                           ALU.mult, ALU.add).then_inc(s_done, 1)
            with dve.If(dense != 0):
                for c in range(TC):
                    tokens_rest(c)
                for k in range(KF):
                    hidden_rest(k)
                for e in range(NE):
                    if e + 2 < NE:
                        weights_rest(e + 2)
                    for c in range(TC):
                        i = e * TC + c
                        dve.wait_ge(s_down, i + 1)
                        if e:
                            dve.wait_ge(s_acc, i - TC + 1)
                        v.scalar_tensor_tensor(x_sb[:, c], bank[4 + i % 4][:, 0:D], gate[:, c, e:e + 1], x_sb[:, c],
                                               ALU.mult, ALU.add).then_inc(s_acc, 1)
                        if e + 1 < NE and c < KF:
                            hidden_rest(KF * (e + 1) + c)

        @block.scalar
        def _(act):
            act.wait_ge(s_edge_pad, 2)
            load_edges(act, 1, dst)
            def swept(i):
                if i >= SWEPT:
                    act.wait_ge(s_sum if i - SWEPT < CH else s_square, (i - SWEPT) % CH + 1)
                return sweep[:, i % SWEPT]

            act.wait_ge(s_const, NCONST)
            nc.scalar.activation(table_use[:, :], one[:, :], ACT.Sqrt)
            for c in range(CH):
                act.wait_ge(s_x[c], 16)
                nc.scalar.activation(swept(c), x_sb[:, c], ACT.Identity, accum_out=sums[:, 0, c:c + 1]).then_inc(s_sum, 1)
            act.wait_ge(s_mean, 1)
            for c in range(CH):
                nc.scalar.activation(swept(CH + c), x_sb[:, c], ACT.Square, bias=neg_mean[:, c:c + 1],
                                     accum_out=sums[:, 1, c:c + 1]).then_inc(s_square, 1)

            def normalise(c):
                if c >= 2:
                    act.wait_ge(s_xnT, c - 1)
                nc.scalar.activation(xn[:, c % 2], x_sb[:, c], ACT.Identity, scale=rstd[:, 0, c:c + 1],
                                     bias=rstd[:, 1, c:c + 1]).then_inc(s_xn, 1)

            def keep_transposed(c):
                act.wait_ge(s_xnT, c + 1)
                nc.scalar.copy(xnt[:, :, c * P:(c + 1) * P],
                               bank[4 + c % 2][:, :].rearrange("p (k n) -> p k n", k=KD)).then_inc(s_xnt, 1)

            def keep_h(c):
                act.wait_ge(s_h, c + 1)
                nc.scalar.copy(h_sb[:, c], bank[6 + c % 2][:, 0:HID]).then_inc(s_hsb, 1)

            def columns(b, n, wide=WIDE):
                return nc.values_load_multi_w_load_instructions(
                    column_i[0:1, bass.ds(b, n)], engines=[act.engine], min_val=0, max_val=NP - wide,
                    skip_runtime_bounds_check_because="columns are kept in the matrix when they are made")[1]

            def place(b, j, column, wide=WIDE):
                act.wait_ge(s_summed, b + 1)
                if not (isinstance(b, int) and b == 0):
                    act.wait_ge(s_placed, b)
                nc.scalar.copy(at[:, :, bass.ds(column, wide)],
                               bank[j][:, 0:CH * wide].rearrange("p (c n) -> p c n", c=CH)).then_inc(s_placed, 1)

            act.wait_ge(s_square, CH)
            nc.scalar.activation(rstd[:, 1], sums[:, 1], ACT.Sqrt, scale=1.0 / D, bias=eps[:, :]).then_inc(s_std, 1)
            act.wait_ge(s_first, 4)
            act.wait_ge(s_at_zero, 1)
            for b in range(HEAD):
                if b % BUILD_BANKS == 0:
                    column = columns(b, BUILD_BANKS)
                place(b, b % BUILD_BANKS, column[b % BUILD_BANKS])
                c, half = divmod(b - FEATURES, 2)
                if b == FEATURES - 1:
                    act.wait_ge(s_rstd, 1)
                    normalise(0)
                elif 0 <= c < CH and half == 0:
                    keep_transposed(c)
                    if c + 1 < CH:
                        normalise(c + 1)
                elif 0 <= c < CH:
                    keep_h(c)
            with act.Fori(0, (FULL_BATCHES - HEAD) // BUILD_BANKS) as it:
                column = columns(it * BUILD_BANKS + HEAD, BUILD_BANKS)
                for j in range(BUILD_BANKS):
                    place(it * BUILD_BANKS + (HEAD + j), j, column[j])
            place(FULL_BATCHES, FULL_BATCHES % BUILD_BANKS, columns(FULL_BATCHES, 1, WIDE_LAST)[0], WIDE_LAST)

            slow = is_slow(act)
            with act.If(slow != 0):
                with act.Fori(0, NWIN) as w:
                    act.wait_ge(s_gen_sum, w + 1)
                    nc.scalar.copy(at[:, :, bass.ds(w * WINDOW, WINDOW)],
                                   bank[0][:, 0:COLS].rearrange("p (c n) -> p c n", c=CH)).then_inc(s_gen_at, 1)

            act.wait_ge(s_deg, 1)
            nc.scalar.activation(std_col[:, :], bank[3][:, 0:CH], ACT.Sqrt, bias=one[:, :]).then_inc(s_deg_std, 1)
            act.wait_ge(s_dinv, 1)
            act.wait_ge(s_hsb, CH)
            for c in range(CH):
                nc.scalar.activation(part[:, 0, c], h_sb[:, c], ACT.Copy, scale=dinv_col[:, c:c + 1]).then_inc(s_p0, 1)
            for i, (a, b) in enumerate(HALVES):
                act.wait_ge(s_r0, i + 1)
                nc.scalar.copy(part[:, 1, a:b], rest[:, a:b]).then_inc(s_p1, 1)
            for i, (a, n) in enumerate(SPANS):
                act.wait_ge(s_dinvT, i + 1)
                nc.scalar.copy(dinv_row[:, a:a + n], bank[i][:, 0:n]).then_inc(s_dinv_row, 1)

            def finish_h1(i):
                a, n = SPANS[i]
                act.wait_ge(s_agg1s, i + 1)
                nc.scalar.activation(h1t[:, a:a + n], h1t[:, a:a + n], ACT.Relu, bias=b1_sb[:, :]).then_inc(s_h1t, 1)

            def first_h2(i):
                a, b = CHUNKS[i]
                act.wait_ge(s_g2, i + 1)
                nc.scalar.copy(part2[:, a:b, 0:LAT], h_sb[:, a:b, 0:LAT]).then_inc(s_q0, 1)

            def second_h2(i):
                a, b = CHUNKS[i]
                act.wait_ge(s_q0r, i + 1)
                nc.scalar.copy(part2[:, a:b, LAT:2 * LAT], rest2[:, a:b]).then_inc(s_q1, 1)

            finish_h1(0)
            finish_h1(1)
            first_h2(0)
            finish_h1(2)
            second_h2(0)
            first_h2(1)
            first_h2(2)
            second_h2(1)
            second_h2(2)

            def finish_z(i):
                a, n = SPANS[i]
                act.wait_ge(s_agg2s, i + 1)
                nc.scalar.activation(zt[:, a:a + n], zt[:, a:a + n], ACT.Identity, bias=b2_sb[:, :]).then_inc(s_zt, 1)

            def finish_y1(i):
                a, n = SPANS[i]
                act.wait_ge(s_d1, i + 1)
                nc.scalar.activation(y1t[:, a:a + n], bank[D1_BANK[i]][:, 0:n], ACT.Relu, bias=bd1_sb[:, :]).then_inc(s_y1, 1)

            def finish_y2(i):
                a, n = SPANS[i]
                for k in range(2):
                    act.wait_ge(s_d2, 2 * i + k + 1)
                    nc.scalar.activation(y2t[:, k, a:a + n], bank[k][:, 0:n], ACT.Relu, bias=bd2_sb[:, k:k + 1]).then_inc(s_y2, 1)

            def normalise_tokens(c):
                nc.scalar.activation(normal(c), x_sb[:, c], ACT.Identity, scale=rstd[:, 0, c:c + 1],
                                     bias=rstd[:, 1, c:c + 1]).then_inc(s_xn2, 1)

            def keep_tokens(c):
                act.wait_ge(s_xn2T, c + 1)
                nc.scalar.copy(xn2t[:, :, c * P:(c + 1) * P],
                               bank[2 + c % 2][:, :].rearrange("p (k n) -> p k n", k=KD)).then_inc(s_xn2t, 1)

            dense, sparse = is_path(act, 0), is_path(act, 1)
            finish_z(0)
            finish_y1(0)
            finish_z(1)
            finish_y2(0)
            finish_z(2)
            finish_y1(1)
            finish_y1(2)
            finish_y2(1)
            act.wait_ge(s_mv2, 1)
            nc.scalar.activation(rstd[:, 1, 0:TC], mv[:, 0:TC, 1], ACT.Sqrt, bias=eps[:, :]).then_inc(s_std2, 1)
            act.wait_ge(s_rstd2, 1)
            for c in range(0, TC, 2):
                normalise_tokens(c)
            finish_y2(2)
            with act.If(sparse != 0):
                def keep_gathered(e):
                    if e >= 2:
                        act.wait_ge(s_up_sp, KF * (e - 1))
                    for i in range(2):
                        act.wait_ge(s_xgT, 2 * e + i + 1)
                        nc.scalar.copy(xg_t[:, e % 2, 2 * i:2 * i + 2, 0],
                                       bank[i][:, 0:2 * SLOTS].rearrange("p (k t) -> p k t", k=2)).then_inc(s_xg_hi, 1)

                def first_parts(e):
                    if e >= W_HI + 1:
                        act.wait_ge(s_down_sp, 2 * (e - W_HI))
                    for w, hi in zip(weights(e), weights_hi(e, W_HI + 1)):
                        nc.scalar.copy(hi, w).then_inc(s_whi_act, 1)

                def keep_part(e):
                    for m in range(KF):
                        act.wait_ge(s_up_sp, KF * e + m + 1)
                        if e >= 1:
                            act.wait_ge(s_hs_sum, KF * (e - 1) + m + 1)
                        nc.scalar.copy(hs_part[:, m], bank[2 + m][:, SLOTS:2 * SLOTS]).then_inc(s_hs_part, 1)

                def keep_more_results(e):
                    act.wait_ge(s_down_sp, 2 * e + 2)
                    if e >= 2:
                        act.wait_ge(s_y_stored[e % 2], 32 * (e // 2))
                    nc.scalar.copy(y_out[0:MORE, e % 2, 1], bank[5 + 2 * (e % 2)][0:MORE, 0:D]).then_inc(s_y_more, 1)

                act.wait_ge(s_ew, 16 * 2 * NE)
                first_parts(2)
                keep_gathered(0)
                keep_gathered(1)
                keep_part(0)
                for e in range(NE):
                    act.wait_ge(s_hs_sum, KF * (e + 1))
                    nc.scalar.activation(hs_raw, hs_raw, ACT.Gelu).then_inc(s_gelu_sp, 1)
                    act.wait_ge(s_gelu_sp, e + 1)
                    if e >= 2:
                        act.wait_ge(s_down_sp, 2 * (e - 1))
                    nc.scalar.copy(hs[:, e % 2, 0], hs_raw).then_inc(s_hs_hi, 1)
                    if e >= 1:
                        keep_more_results(e - 1)
                    if e + 3 < NE:
                        first_parts(e + 3)
                    if e + 2 < NE:
                        keep_gathered(e + 2)
                    if e + 1 < NE:
                        keep_part(e + 1)
                keep_more_results(NE - 1)
            with act.If(dense != 0):
                for c in range(TC):
                    keep_tokens(c)
                for e in range(NE):
                    for k in range(KF):
                        i = KF * e + k
                        act.wait_ge(s_up, i + 1)
                        if i >= H_RAW:
                            act.wait_ge(s_hlo, i - H_RAW + 1)
                        nc.scalar.activation(h_raw[:, i % H_RAW], bank[i % 4][:, 0:T], ACT.Gelu).then_inc(s_gelu, 1)
                        act.wait_ge(s_gelu, i + 1)
                        if e >= 2:
                            act.wait_ge(s_down, TC * (e - 1))
                        nc.scalar.copy(hidden[:, e % 2, 0, k], h_raw[:, i % H_RAW]).then_inc(s_hhi, 1)

        @block.tensor
        def _(pe):
            mm = nc.tensor.matmul
            pe.wait_ge(s_const, NCONST)
            for i in range(WARM):
                mm(bank[7][:, 0:COLS], ones_bf[:, :], zeros_bf[:, :], start=True, stop=True)
            pe.wait_ge(s_rows, 1)
            for k in range(2):
                for t in range(ROWT):
                    nc.tensor.transpose(bank[k][:, t * ROWS:(t + 1) * ROWS], frow[:, k, t * P:(t + 1) * P], ident[0:ROWS, 0:ROWS])
            for k in range(4):
                o = bank[2 + k // 3][:, (k % 3) * GROUPS:(k % 3 + 1) * GROUPS].rearrange("p (r h) -> p h r", h=ROWG)
                for h in range(ROWG):
                    last = mm(o[:, h], gstat[0:ROWS, k, h:h + 1].to_broadcast([ROWS, P]), ident[0:ROWS, 0:ROWS],
                              start=True, stop=True)
            last.then_inc(s_rowT, 1)

            def transpose_features(c):
                pe.wait_ge(s_xn, c + 1)
                if c >= 2:
                    pe.wait_ge(s_xnt, c - 1)
                for k in range(KD):
                    last = nc.tensor.transpose(bank[4 + c % 2][:, k * P:(k + 1) * P], xn[:, c % 2, k * P:(k + 1) * P], ident[:, :])
                last.then_inc(s_xnT, 1)

            def project(c):
                if c == 0:
                    pe.wait_ge(s_wg, 16 * NWG)
                pe.wait_ge(s_xnt, c + 1)
                if c >= 2:
                    pe.wait_ge(s_hsb, c - 1)
                for k in range(KD):
                    last = mm(bank[6 + c % 2][:, 0:HID], xnt[:, k, c * P:(c + 1) * P], w1t_sb[:, k],
                              start=(k == 0), stop=(k == KD - 1))
                last.then_inc(s_h, 1)

            def sum_batch(b, j, wide=WIDE, groups=BG):
                _, shifts = nc.values_load_multi_w_load_instructions(
                    shift_i[0:1, bass.ds(b * BG, groups)], engines=[pe.engine], min_val=0, max_val=wide - WINDOW,
                    skip_runtime_bounds_check_because="shifts are kept in the window when they are made")
                pe.wait_ge(s_ready, b + 1)
                if not (isinstance(b, int) and b < BUILD_BANKS):
                    pe.wait_ge(s_placed, b - BUILD_BANKS + 1)
                acc = bank[j][:, 0:CH * wide]
                mm(acc, ident_bf[:, :], zeros_bf[:, 0:1].to_broadcast([P, CH * wide]), start=True, stop=False)
                acc = acc.rearrange("p (c n) -> p c n", n=wide)
                first = isinstance(b, int) and b == 0
                for g in range(groups):
                    for t in range(g * GROUP, (g + 1) * GROUP):
                        last = mm(acc[:, :, bass.ds(shifts[g], WINDOW)], hot_src[:, j, t], hot_dst[:, j, t],
                                  start=False, stop=(first and t == BATCH - 1))
                if not first:
                    if isinstance(b, int) and b == 1:
                        pe.wait_ge(s_carry, 1)
                    last = mm(acc[:, :, 0], hot_src[:, (j - 1) % RING, BATCH - 1],
                              hot_carry[:, bass.ds(b - 1, 1)].rearrange("p a c -> p (a c)"), start=False, stop=True)
                last.then_inc(s_summed, 1)

            pe.wait_ge(s_first, 4)
            for b in range(HEAD):
                if b == 3:
                    pe.wait_ge(s_slow, 1)
                sum_batch(b, b % BUILD_BANKS)
                c, half = divmod(b - FEATURES, 2)
                if 0 <= c < CH:
                    if half == 0:
                        transpose_features(c)
                    else:
                        project(c)
            with pe.Fori(0, (FULL_BATCHES - HEAD) // BUILD_BANKS) as it:
                for j in range(BUILD_BANKS):
                    sum_batch(it * BUILD_BANKS + (HEAD + j), j)
            sum_batch(FULL_BATCHES, FULL_BATCHES % BUILD_BANKS, WIDE_LAST, LAST_GROUPS)

            slow = is_slow(pe)
            pe.wait_ge(s_placed, NBATCH)
            with pe.If(slow != 0):
                pe.wait_ge(s_gen_begin, 2)
                pe.sem_inc(s_gen_used, 1)
                pe.sem_inc(s_gen_free, 1)
                with pe.Fori(0, NWIN) as w:
                    pe.wait_ge(s_gen_free, w + 1)
                    mm(bank[0][:, 0:COLS], ident_bf[:, :], zeros_bf[:, :], start=True, stop=False)
                    with pe.Fori(0, NBATCH) as b:
                        pe.wait_ge(s_gen_ready, w * NBATCH + b + 1)
                        for t in range(BATCH):
                            last = mm(bank[0][:, 0:COLS], hot_src[:, 0, t], hot_dst[:, 0, t], start=False, stop=False)
                        last.then_inc(s_gen_used, 1)
                    mm(bank[0][:, 0:COLS], ident_bf[:, :], zeros_bf[:, :], start=False, stop=True).then_inc(s_gen_sum, 1)
                    pe.wait_ge(s_gen_at2, w + 1)
                    pe.sem_inc(s_gen_free, 1)

            def degrees(counts):
                for c in range(CH):
                    for s in range(CH):
                        mm(bank[3][:, c:c + 1], counts[:, s, c * P:(c + 1) * P], ones_bf[:, 0:1],
                           start=False, stop=False)

            mm(bank[3][:, 0:CH], ident_bf[:, :], zeros_bf[:, 0:CH], start=True, stop=False)
            degrees(at)
            with pe.If(slow != 0):
                degrees(at2)
            mm(bank[3][:, 0:CH], ident_bf[:, :], zeros_bf[:, 0:CH], start=False, stop=True).then_inc(s_deg, 1)
            pe.wait_ge(s_dinv, 1)
            for i, (a, b) in enumerate(CHUNKS):
                for c in range(a, b):
                    last = mm(bank[i][:, (c - a) * P:(c - a + 1) * P], dinv_col[:, c:c + 1].to_broadcast([P, P]), ident[:, :],
                              start=True, stop=True)
                last.then_inc(s_dinvT, 1)

            def neighbours(parts, wait_part, done, after_span, before_last=None):
                def add(counts, k, s, spans):
                    for i in spans:
                        a, n = SPANS[i]
                        mm(bank[4 + i][:, 0:n], parts[k][:, s], counts[:, s, a:a + n],
                           start=(counts is at and k == 0 and s == 0), stop=False)

                def add_own(k, c, stop=False):
                    i = c * P // 512
                    return mm(bank[4 + i][:, c * P - SPANS[i][0]:(c + 1) * P - SPANS[i][0]], parts[k][:, c], ident_bf[:, :],
                              start=False, stop=stop)

                last_k = len(parts) - 1
                for k in range(last_k):
                    for s in range(CH):
                        wait_part(k, s)
                        add(at, k, s, range(len(SPANS)))
                        if k or s:
                            add_own(k, s)
                    if k == 0:
                        add_own(k, 0)
                        with pe.If(slow != 0):
                            for kk in range(len(parts)):
                                for s in range(CH):
                                    wait_part(kk, s)
                                    add(at2, kk, s, range(len(SPANS)))
                if before_last:
                    before_last()
                for i, (a, b) in enumerate(CHUNKS):
                    for s in range(CH):
                        wait_part(last_k, s)
                        add(at, last_k, s, [i])
                    for c in range(a, b):
                        last = add_own(last_k, c, stop=(c == b - 1))
                    last.then_inc(done, 1)
                    after_span(i)

            def wait_part1(k, s):
                if k == 0:
                    pe.wait_ge(s_p0, s + 1)
                else:
                    pe.wait_ge(s_p1 if k == 1 else s_p2, 1 if s < HALF else 2)

            def product_h2(i):
                a, b = CHUNKS[i]
                pe.wait_ge(s_h1t, i + 1)
                if i == 2:
                    pe.wait_ge(s_g2, 1)
                for c in range(a, b):
                    last = mm(bank[H2_BANK[i]][:, (c - a) * LAT:(c - a + 1) * LAT], h1t[:, c * P:(c + 1) * P], w2t_sb[:, :],
                              start=True, stop=True)
                last.then_inc(s_h2, 1)

            def rank_assignments():
                pe.wait_ge(s_chosen, 1)
                mm(bank[7][:, 0:(J + 1) * NE], before[:, :], chosen[:, :, :].rearrange("p j e -> p (j e)"), start=True, stop=False)
                for j in range(J):
                    last = mm(bank[7][:, (j + 1) * NE:(J + 1) * NE].rearrange("p (a e) -> p a e", e=NE), ones_bf[:, :],
                              chosen[:, j:j + 1].to_broadcast([P, J - j, NE]), start=False, stop=(j == J - 1))
                last.then_inc(s_ranks, 1)

            def rows_of_slots():
                pe.wait_ge(s_rank_hot, J + 1)
                for a, b, at_col in ((0, P, 0), (P, SLOTS, NE)):
                    for j in range(J):
                        last = mm(bank[0][0:b - a, at_col:at_col + NE], rank_hot[:, j, a:b], chosen_token[:, j],
                                  start=(j == 0), stop=(j == J - 1))
                last.then_inc(s_rows_sum, 1)

            neighbours([part[:, 0], part[:, 1], part[:, 2]], wait_part1, s_agg1,
                       lambda i: product_h2(0) if i == 1 else None, before_last=rank_assignments)
            product_h2(1)
            product_h2(2)
            dense, sparse = is_path(pe, 0), is_path(pe, 1)
            pe.wait_ge(s_dinv_row, len(SPANS))
            rows_of_slots()

            def wait_part2(k, s):
                span = s * P // 512
                if k == 0:
                    pe.wait_ge(s_q1, span + 1)
                else:
                    pe.wait_ge(s_q2, span + 1)
                    pe.wait_ge(s_q2_pad, 1)

            def decode1(i):
                a, n = SPANS[i]
                pe.wait_ge(s_zt, i + 1)
                if i == 2:
                    pe.wait_ge(s_y1, 1)
                mm(bank[D1_BANK[i]][:, 0:n], wd1t_sb[:, :], zt[:, a:a + n], start=True, stop=True).then_inc(s_d1, 1)

            def decode2(i):
                a, n = SPANS[i]
                pe.wait_ge(s_y1, i + 1)
                for k in range(2):
                    if i >= 1:
                        pe.wait_ge(s_y2, 2 * (i - 1) + k + 1)
                    mm(bank[k][:, 0:n], wd2t_sb[:, k * P:(k + 1) * P], y1t[:, a:a + n], start=True, stop=True).then_inc(s_d2, 1)

            def decode3(c):
                pe.wait_ge(s_y2, 2 * (c * P // 512) + 2)
                if c == 0:
                    pe.wait_ge(s_agg2s, len(SPANS))
                if c >= 4:
                    pe.wait_ge(s_x2, c - 3)
                for k in range(2):
                    last = mm(bank[4 + c % 4][:, 0:D], y2t[:, k, c * P:(c + 1) * P], wd3t_sb[:, k], start=(k == 0), stop=(k == 1))
                last.then_inc(s_d3, 1)

            def transpose_tokens(c):
                pe.wait_ge(s_xn2_odd if c % 2 else s_xn2, c // 2 + 1)
                if c < 2:
                    pe.wait_ge(s_y1, 3)
                else:
                    pe.wait_ge(s_xn2l, c - 1)
                for k in range(KD):
                    last = nc.tensor.transpose(bank[2 + c % 2][:, k * P:(k + 1) * P], normal(c)[:, k * P:(k + 1) * P], ident[:, :])
                last.then_inc(s_xn2T, 1)

            neighbours([part2, part3], wait_part2, s_agg2, lambda i: decode1(0) if i == 1 else None)
            decode2(0)
            decode1(1)
            for c in range(CH):
                if c == TC - 1:
                    decode2(1)
                decode3(c)
                if c == 0:
                    decode1(2)
                if c == TC:
                    decode2(2)

            def product(acc, lhs, rhs, cuts):
                passes = [(k, a, b) for k in range(cuts) for a, b in ((0, 0), (0, 1), (1, 0))]
                for i, (k, a, b) in enumerate(passes):
                    last = mm(acc, lhs(a, k), rhs(b, k), start=(i == 0), stop=(i == len(passes) - 1))
                return last

            with pe.If(sparse != 0):
                def transpose_gathered(e):
                    pe.wait_ge(s_gathered[e % XG], 32 * (e // XG + 1))
                    for i in range(2):
                        if e >= 1:
                            pe.wait_ge(s_xg_lo, 2 * (e - 1) + i + 1)
                        for k in range(2 * i, 2 * i + 2):
                            o = (k - 2 * i) * SLOTS
                            nc.tensor.transpose(bank[i][:, o:o + P], xg[:, e % XG, 0, k * P:(k + 1) * P], ident[:, :])
                            last = nc.tensor.transpose(bank[i][:, o + P:o + SLOTS], xg[0:MORE, e % XG, 1, k * P:(k + 1) * P],
                                                       ident[0:MORE, 0:MORE])
                        last.then_inc(s_xgT, 1)

                def up_slots(e):
                    w1_hi = weights_hi(e, W_HI + 1)[0].rearrange("p (k n) -> p k n", k=KD)
                    pe.wait_ge(s_wlo, 2 * (e + 1))
                    pe.wait_ge(s_xg_lo, 2 * (e + 1))
                    for m in range(KF):
                        if e >= 1:
                            pe.wait_ge(s_hs_sum, KF * (e - 1) + m + 1)
                        acc = bank[2 + m]
                        for k in range(KD):
                            mm(acc[:, 0:2 * SLOTS], w1_hi[:, k, m * P:(m + 1) * P],
                               xg_t[:, e % 2, k].rearrange("p h t -> p (h t)"), start=(k == 0), stop=False)
                        for k in range(KD):
                            last = mm(acc[:, 0:SLOTS], w1_lo[:, e, k, m * P:(m + 1) * P], xg_t[:, e % 2, k, 0],
                                      start=False, stop=(k == KD - 1))
                        last.then_inc(s_up_sp, 1)

                def down_slots(e):
                    w2_hi = weights_hi(e, W_HI + 1)[1].rearrange("p (k n) -> p k n", k=KF)
                    pe.wait_ge(s_hs_lo, e + 1)
                    for i, (a, b) in enumerate(((0, P), (P, SLOTS))):
                        if e >= 2:
                            pe.wait_ge(s_y_more if i else s_y, e - 1)
                        product(bank[4 + 2 * (e % 2) + i][0:b - a, 0:D], lambda h, k: hs[:, e % 2, h, k, a:b],
                                lambda h, k: (w2_lo[:, e] if h else w2_hi)[:, k], KF).then_inc(s_down_sp, 1)

                pe.wait_ge(s_x2, CH)
                transpose_gathered(0)
                transpose_gathered(1)
                up_slots(0)
                for e in range(NE):
                    if e + 1 < NE:
                        up_slots(e + 1)
                    if e + 2 < NE:
                        transpose_gathered(e + 2)
                    down_slots(e)
            with pe.If(dense != 0):
                for c in range(TC):
                    transpose_tokens(c)
                pe.wait_ge(s_xn2l, TC)
                pe.wait_ge(s_x2, CH)

                def up(e):
                    w1_hi = weights_hi(e)[0].rearrange("p (k n) -> p k n", k=KD)
                    pe.wait_ge(s_wlo, 2 * (e + 1))
                    for m in range(KF):
                        i = KF * e + m
                        if i >= 4:
                            pe.wait_ge(s_gelu, i - 3)
                        product(bank[i % 4][:, 0:T], lambda a, k: (w1_lo[:, e] if a else w1_hi)[:, k, m * P:(m + 1) * P],
                                lambda b, k: (xn2t_lo if b else xn2t)[:, k], KD).then_inc(s_up, 1)

                up(0)
                for e in range(NE):
                    if e + 1 < NE:
                        up(e + 1)
                    w2_hi = weights_hi(e)[1].rearrange("p (k n) -> p k n", k=KF)
                    pe.wait_ge(s_hlo, KF * (e + 1))
                    for c in range(TC):
                        i = e * TC + c
                        if i >= 4:
                            pe.wait_ge(s_acc, i - 3)
                        product(bank[4 + i % 4][:, 0:D], lambda a, k: hidden[:, e % 2, a, k, c * P:(c + 1) * P],
                                lambda b, k: (w2_lo[:, e] if b else w2_hi)[:, k], KF).then_inc(s_down, 1)

def kernel(x, src, dst, L0_gnn_W1, L0_gnn_b1, L0_gnn_W2, L0_gnn_b2, L0_gnn_Wd1, L0_gnn_bd1, L0_gnn_Wd2,
           L0_gnn_bd2, L0_gnn_Wd3, L0_gnn_bd3, L0_ffn_expert_weights, L0_ffn_expert_indices, L0_ffn_w1,
           L0_ffn_w2):
    import numpy as np
    import concourse.bacc as bacc
    from concourse.bass_utils import run_bass_kernel_spmd

    nc = bacc.Bacc("TRN2", target_bir_lowering=False, num_devices=1)
    given = dict(
        x=x, src=src, dst=dst,
        W1T=np.asarray(L0_gnn_W1).T, b1=L0_gnn_b1, W2T=np.asarray(L0_gnn_W2).T, b2=L0_gnn_b2,
        Wd1T=np.asarray(L0_gnn_Wd1).T, bd1=L0_gnn_bd1,
        Wd2T=np.asarray(L0_gnn_Wd2).T, bd2=np.asarray(L0_gnn_bd2).reshape(-1, P).T,
        Wd3T=np.asarray(L0_gnn_Wd3).T, bd3=L0_gnn_bd3,
        gate_w=L0_ffn_expert_weights, gate_i=L0_ffn_expert_indices, w1=L0_ffn_w1, w2=L0_ffn_w2)
    arrays, args = {}, {}
    for name, a in given.items():
        a = np.ascontiguousarray(a)
        arrays[f"in_{name}"] = a
        args[name] = nc.dram_tensor(f"in_{name}", a.shape, mybir.dt.from_np(a.dtype), kind="ExternalInput").ap()
    out = nc.dram_tensor("out", arrays["in_x"].shape, F32, kind="ExternalOutput").ap()
    gnn_moe(nc, **args, out=out)
    r = run_bass_kernel_spmd(nc, [arrays], core_ids=[0])
    return r.results[0]["out"]
```
